# Optimizing a Trainium2 kernel written in Bass

```python
import numpy as np
import jax
import jax.numpy as jnp

def _softmax(x, axis=-1):
    return jax.nn.softmax(x, axis=axis)

def _gelu(x):
    return jax.nn.gelu(x, approximate=True)

def _silu(x):
    return jax.nn.silu(x)

def _sigmoid(x):
    return jax.nn.sigmoid(x)

def _layernorm(x, axis=-1, eps=1e-05):
    m = jnp.mean(x, axis=axis, keepdims=True)
    v = jnp.var(x, axis=axis, keepdims=True)
    return (x - m) / jnp.sqrt(v + eps)

def _scatter_add(tgt, idx, src, axis=0):
    return tgt.at[idx].add(src)

def _segment_sum(src, seg, n):
    return jax.ops.segment_sum(src, seg, n)
kernel_name = 'mk_adaln_ffn_d2_seqx_r4_f05c13'

def setup_inputs(seed: int=0):
    np.random.seed(seed)
    _w = jnp.asarray

    def _rec_inputs():
        import jax
        import jax.numpy as jnp
        _rk = jax.random.key(seed)
        x = -0.000125 + 0.9999 * jax.random.normal(jax.random.fold_in(_rk, 1), (4, 512, 512), jnp.float32)
        _lenS = 512 - jax.random.randint(jax.random.fold_in(_rk, 7), (4,), 0, max(1, 512 // 4) + 1, jnp.int32)
        _lenS2 = 512 - jax.random.randint(jax.random.fold_in(_rk, 8), (4,), 0, max(1, 512 // 4) + 1, jnp.int32)
        fside_BxSxS_0 = -1.52775e-05 + 0.999936 * jax.random.normal(jax.random.fold_in(_rk, 11), (4, 512, 512), jnp.float32)
        cond_512 = -5.03954e-05 + 1.00559 * jax.random.normal(jax.random.fold_in(_rk, 12), (4, 128), jnp.float32)
        return (x, fside_BxSxS_0, cond_512)
    x, fside_BxSxS_0, cond_512 = _rec_inputs()

    def _L0_cond_setup():
        import jax, jax.numpy as jnp
        from jax import lax
        import numpy as np
        B, T, C, TD = (8, 512, 512, 128)

        def _bi_wkv(r, k, v, w, u, time_emb):
            tf = jax.nn.sigmoid(jnp.sum(time_emb, axis=-1))[:, None, None]
            decay = jnp.exp(-jnp.exp(w.astype(jnp.float32)))[None, :] * (0.5 + 0.5 * tf[:, :, 0])
            kf = k.astype(jnp.float32)
            vf = v.astype(jnp.float32)
            ek = jnp.exp(jnp.minimum(kf, 30.0))
            ekv = ek * vf

            def step(carry, x):
                a, b = carry
                ekv_t, ek_t = x
                a = a * decay + ekv_t
                b = b * decay + ek_t
                return ((a, b), (a, b))
            ekv_t = jnp.swapaxes(ekv, 0, 1)
            ek_t = jnp.swapaxes(ek, 0, 1)
            init = (jnp.zeros_like(decay), jnp.zeros_like(decay))
            _, (nf, df) = lax.scan(step, init, (ekv_t, ek_t))
            _, (nb, db) = lax.scan(step, init, (ekv_t, ek_t), reverse=True)
            nf = jnp.swapaxes(nf, 0, 1)
            df = jnp.swapaxes(df, 0, 1)
            nb = jnp.swapaxes(nb, 0, 1)
            db = jnp.swapaxes(db, 0, 1)
            euk = jnp.exp(jnp.minimum(u.astype(jnp.float32)[None, None, :] + kf, 30.0))
            num = nf + nb - ekv + euk * vf
            den = df + db - ek + euk
            base = jax.nn.sigmoid(r.astype(jnp.float32)) * (num / jnp.maximum(den, 1e-08))
            out = base * (0.8 + 0.2 * tf)
            return out.astype(r.dtype)
        key = jax.random.key(seed)
        ks = jax.random.split(key, 6)
        return {'r': jax.random.normal(ks[0], (B, T, C), dtype=jnp.float32), 'k': jax.random.normal(ks[1], (B, T, C), dtype=jnp.float32), 'v': jax.random.normal(ks[2], (B, T, C), dtype=jnp.float32), 'w': jax.random.normal(ks[3], (C,), dtype=jnp.float32), 'u': jax.random.normal(ks[4], (C,), dtype=jnp.float32), 'time_emb': jax.random.normal(ks[5], (B, TD), dtype=jnp.float32)}
    _L0_cond_all = _L0_cond_setup()
    _L0_cond_in = {k: v for k, v in _L0_cond_all.items() if k in ('w', 'u')}
    del _L0_cond_all

    def _L0_ffn_setup():
        import jax, jax.numpy as jnp
        import numpy as np
        _FP8_MAX = 448.0
        _BLOCK = 32
        _EPS = 1e-30

        def _mx_dequant(t):
            rows, feat = t.shape
            blocks = t.reshape(rows, feat // _BLOCK, _BLOCK)
            max_abs = jnp.max(jnp.abs(blocks), axis=-1)
            scales = jnp.maximum(max_abs / _FP8_MAX, _EPS)
            q = (blocks / scales[..., None]).astype(jnp.float8_e4m3fn).astype(jnp.float32)
            return (q * scales[..., None]).reshape(rows, feat)

        def _mx_linear(x2d, w):
            return _mx_dequant(x2d) @ _mx_dequant(w).T
        key = jax.random.key(seed)
        k1, k2, k3, k4 = jax.random.split(key, 4)
        B, S, H, I = (2, 256, 512, 2048)
        return {'x': jax.random.normal(k1, (B, S, H), dtype=jnp.float32), 'gate_w': jax.random.normal(k2, (I, H), dtype=jnp.float32) * 0.02, 'up_w': jax.random.normal(k3, (I, H), dtype=jnp.float32) * 0.02, 'down_w': jax.random.normal(k4, (H, I), dtype=jnp.float32) * 0.02}
    _L0_ffn_all = _L0_ffn_setup()
    _L0_ffn_in = {k: v for k, v in _L0_ffn_all.items() if k in ('gate_w', 'up_w', 'down_w')}
    del _L0_ffn_all

    def _L1_cond_setup():
        import jax, jax.numpy as jnp
        from jax import lax
        import numpy as np
        B, T, C, TD = (8, 512, 512, 128)

        def _bi_wkv(r, k, v, w, u, time_emb):
            tf = jax.nn.sigmoid(jnp.sum(time_emb, axis=-1))[:, None, None]
            decay = jnp.exp(-jnp.exp(w.astype(jnp.float32)))[None, :] * (0.5 + 0.5 * tf[:, :, 0])
            kf = k.astype(jnp.float32)
            vf = v.astype(jnp.float32)
            ek = jnp.exp(jnp.minimum(kf, 30.0))
            ekv = ek * vf

            def step(carry, x):
                a, b = carry
                ekv_t, ek_t = x
                a = a * decay + ekv_t
                b = b * decay + ek_t
                return ((a, b), (a, b))
            ekv_t = jnp.swapaxes(ekv, 0, 1)
            ek_t = jnp.swapaxes(ek, 0, 1)
            init = (jnp.zeros_like(decay), jnp.zeros_like(decay))
            _, (nf, df) = lax.scan(step, init, (ekv_t, ek_t))
            _, (nb, db) = lax.scan(step, init, (ekv_t, ek_t), reverse=True)
            nf = jnp.swapaxes(nf, 0, 1)
            df = jnp.swapaxes(df, 0, 1)
            nb = jnp.swapaxes(nb, 0, 1)
            db = jnp.swapaxes(db, 0, 1)
            euk = jnp.exp(jnp.minimum(u.astype(jnp.float32)[None, None, :] + kf, 30.0))
            num = nf + nb - ekv + euk * vf
            den = df + db - ek + euk
            base = jax.nn.sigmoid(r.astype(jnp.float32)) * (num / jnp.maximum(den, 1e-08))
            out = base * (0.8 + 0.2 * tf)
            return out.astype(r.dtype)
        key = jax.random.key(seed)
        ks = jax.random.split(key, 6)
        return {'r': jax.random.normal(ks[0], (B, T, C), dtype=jnp.float32), 'k': jax.random.normal(ks[1], (B, T, C), dtype=jnp.float32), 'v': jax.random.normal(ks[2], (B, T, C), dtype=jnp.float32), 'w': jax.random.normal(ks[3], (C,), dtype=jnp.float32), 'u': jax.random.normal(ks[4], (C,), dtype=jnp.float32), 'time_emb': jax.random.normal(ks[5], (B, TD), dtype=jnp.float32)}
    _L1_cond_all = _L1_cond_setup()
    _L1_cond_in = {k: v for k, v in _L1_cond_all.items() if k in ('w', 'u')}
    del _L1_cond_all

    def _L1_ffn_setup():
        import jax, jax.numpy as jnp
        import numpy as np
        IN_F, OUT_F = (512, 512)
        N_EXPERTS, RANK, TOP_K = (8, 128, 2)
        key = jax.random.key(seed)
        k_x, k_r, k_a, k_b = jax.random.split(key, 4)
        hidden_states = jax.random.normal(k_x, (4, 1024, IN_F), dtype=jnp.float32)
        router_w = jax.random.normal(k_r, (IN_F, N_EXPERTS), dtype=jnp.float32) * IN_F ** (-0.5)
        Wa = jax.random.normal(k_a, (N_EXPERTS, IN_F, RANK), dtype=jnp.float32) * IN_F ** (-0.5)
        Wb = jax.random.normal(k_b, (N_EXPERTS, RANK, OUT_F), dtype=jnp.float32) * RANK ** (-0.5)
        return {'hidden_states': hidden_states, 'router_w': router_w, 'Wa': Wa, 'Wb': Wb}
    _L1_ffn_all = _L1_ffn_setup()
    _L1_ffn_in = {k: v for k, v in _L1_ffn_all.items() if k in ('router_w', 'Wa', 'Wb')}
    del _L1_ffn_all
    return {'x': x, 'fside_BxSxS_0': fside_BxSxS_0, 'cond_512': cond_512, 'L0_cond_w': _L0_cond_in['w'], 'L0_cond_u': _L0_cond_in['u'], 'L0_ffn_gate_w': _L0_ffn_in['gate_w'], 'L0_ffn_up_w': _L0_ffn_in['up_w'], 'L0_ffn_down_w': _L0_ffn_in['down_w'], 'L1_cond_w': _L1_cond_in['w'], 'L1_cond_u': _L1_cond_in['u'], 'L1_ffn_router_w': _L1_ffn_in['router_w'], 'L1_ffn_Wa': _L1_ffn_in['Wa'], 'L1_ffn_Wb': _L1_ffn_in['Wb']}

def reference(x, fside_BxSxS_0, cond_512, L0_cond_w, L0_cond_u, L0_ffn_gate_w, L0_ffn_up_w, L0_ffn_down_w, L1_cond_w, L1_cond_u, L1_ffn_router_w, L1_ffn_Wa, L1_ffn_Wb):
    import jax
    import jax.numpy as jnp

    def _L0_cond_ref(r, k, v, w, u, time_emb):
        import jax, jax.numpy as jnp
        from jax import lax
        import numpy as np
        B, T, C, TD = (8, 512, 512, 128)

        def _bi_wkv(r, k, v, w, u, time_emb):
            tf = jax.nn.sigmoid(jnp.sum(time_emb, axis=-1))[:, None, None]
            decay = jnp.exp(-jnp.exp(w.astype(jnp.float32)))[None, :] * (0.5 + 0.5 * tf[:, :, 0])
            kf = k.astype(jnp.float32)
            vf = v.astype(jnp.float32)
            ek = jnp.exp(jnp.minimum(kf, 30.0))
            ekv = ek * vf

            def step(carry, x):
                a, b = carry
                ekv_t, ek_t = x
                a = a * decay + ekv_t
                b = b * decay + ek_t
                return ((a, b), (a, b))
            ekv_t = jnp.swapaxes(ekv, 0, 1)
            ek_t = jnp.swapaxes(ek, 0, 1)
            init = (jnp.zeros_like(decay), jnp.zeros_like(decay))
            _, (nf, df) = lax.scan(step, init, (ekv_t, ek_t))
            _, (nb, db) = lax.scan(step, init, (ekv_t, ek_t), reverse=True)
            nf = jnp.swapaxes(nf, 0, 1)
            df = jnp.swapaxes(df, 0, 1)
            nb = jnp.swapaxes(nb, 0, 1)
            db = jnp.swapaxes(db, 0, 1)
            euk = jnp.exp(jnp.minimum(u.astype(jnp.float32)[None, None, :] + kf, 30.0))
            num = nf + nb - ekv + euk * vf
            den = df + db - ek + euk
            base = jax.nn.sigmoid(r.astype(jnp.float32)) * (num / jnp.maximum(den, 1e-08))
            out = base * (0.8 + 0.2 * tf)
            return out.astype(r.dtype)
        return _bi_wkv(r, k, v, w, u, time_emb)

    def _L0_ffn_ref(x, gate_w, up_w, down_w):
        import jax, jax.numpy as jnp
        import numpy as np
        _FP8_MAX = 448.0
        _BLOCK = 32
        _EPS = 1e-30

        def _mx_dequant(t):
            rows, feat = t.shape
            blocks = t.reshape(rows, feat // _BLOCK, _BLOCK)
            max_abs = jnp.max(jnp.abs(blocks), axis=-1)
            scales = jnp.maximum(max_abs / _FP8_MAX, _EPS)
            q = (blocks / scales[..., None]).astype(jnp.float8_e4m3fn).astype(jnp.float32)
            return (q * scales[..., None]).reshape(rows, feat)

        def _mx_linear(x2d, w):
            return _mx_dequant(x2d) @ _mx_dequant(w).T
        B, S, H = x.shape
        x2d = x.reshape(B * S, H)
        gate = _mx_linear(x2d, gate_w)
        up = _mx_linear(x2d, up_w)
        h = jax.nn.silu(gate) * up
        out = _mx_linear(h, down_w)
        return out.reshape(B, S, H)

    def _L1_cond_ref(r, k, v, w, u, time_emb):
        import jax, jax.numpy as jnp
        from jax import lax
        import numpy as np
        B, T, C, TD = (8, 512, 512, 128)

        def _bi_wkv(r, k, v, w, u, time_emb):
            tf = jax.nn.sigmoid(jnp.sum(time_emb, axis=-1))[:, None, None]
            decay = jnp.exp(-jnp.exp(w.astype(jnp.float32)))[None, :] * (0.5 + 0.5 * tf[:, :, 0])
            kf = k.astype(jnp.float32)
            vf = v.astype(jnp.float32)
            ek = jnp.exp(jnp.minimum(kf, 30.0))
            ekv = ek * vf

            def step(carry, x):
                a, b = carry
                ekv_t, ek_t = x
                a = a * decay + ekv_t
                b = b * decay + ek_t
                return ((a, b), (a, b))
            ekv_t = jnp.swapaxes(ekv, 0, 1)
            ek_t = jnp.swapaxes(ek, 0, 1)
            init = (jnp.zeros_like(decay), jnp.zeros_like(decay))
            _, (nf, df) = lax.scan(step, init, (ekv_t, ek_t))
            _, (nb, db) = lax.scan(step, init, (ekv_t, ek_t), reverse=True)
            nf = jnp.swapaxes(nf, 0, 1)
            df = jnp.swapaxes(df, 0, 1)
            nb = jnp.swapaxes(nb, 0, 1)
            db = jnp.swapaxes(db, 0, 1)
            euk = jnp.exp(jnp.minimum(u.astype(jnp.float32)[None, None, :] + kf, 30.0))
            num = nf + nb - ekv + euk * vf
            den = df + db - ek + euk
            base = jax.nn.sigmoid(r.astype(jnp.float32)) * (num / jnp.maximum(den, 1e-08))
            out = base * (0.8 + 0.2 * tf)
            return out.astype(r.dtype)
        return _bi_wkv(r, k, v, w, u, time_emb)

    def _L1_ffn_ref(hidden_states, router_w, Wa, Wb):
        import jax, jax.numpy as jnp
        import numpy as np
        IN_F, OUT_F = (512, 512)
        N_EXPERTS, RANK, TOP_K = (8, 128, 2)
        B, S, D = hidden_states.shape
        x = hidden_states.reshape(-1, D)
        norm = jnp.maximum(jnp.linalg.norm(x, axis=-1, keepdims=True), 1e-12)
        router_logits = x / norm @ router_w
        routing_weights = jax.nn.softmax(router_logits.astype(jnp.float32), axis=-1)
        rw, selected_experts = jax.lax.top_k(routing_weights, TOP_K)
        rw = rw / jnp.sum(rw, axis=-1, keepdims=True)
        rw = rw.astype(hidden_states.dtype)
        combine = jnp.sum(jax.nn.one_hot(selected_experts, N_EXPERTS, dtype=rw.dtype) * rw[..., None], axis=1)
        out = jnp.zeros((x.shape[0], OUT_F), dtype=hidden_states.dtype)
        for e in range(N_EXPERTS):
            out = out + combine[:, e, None] * (x @ Wa[e] @ Wb[e])
        return out.reshape(B, S, OUT_F)
    x = x + _L0_ffn_ref(_L0_cond_ref(x, fside_BxSxS_0, fside_BxSxS_0, L0_cond_w, L0_cond_u, cond_512), L0_ffn_gate_w, L0_ffn_up_w, L0_ffn_down_w)
    x = x + _L1_ffn_ref(_L1_cond_ref(x, fside_BxSxS_0, fside_BxSxS_0, L1_cond_w, L1_cond_u, cond_512), L1_ffn_router_w, L1_ffn_Wa, L1_ffn_Wb)
    return x

_drawn_inputs = setup_inputs


def setup_inputs(seed=0):
    import zlib

    import numpy as np

    out = dict(_drawn_inputs(seed))
    spreads = {}
    factors = {'L0_cond_u': 4.517, 'L0_cond_w': 2.672}
    for name, (base, spread) in spreads.items():
        noise = np.random.default_rng([zlib.crc32(name.encode()), seed]).standard_normal(out[name].shape)
        drawn = base * np.exp(spread * noise) if base else spread * noise
        out[name] = jnp.asarray(drawn.astype(out[name].dtype))
    for name, factor in factors.items():
        out[name] = (out[name] * factor).astype(out[name].dtype)
    return out
```

```python
import math
from contextlib import ExitStack

import numpy as np

import concourse.bass as bass
from concourse import mybir

FP32 = mybir.dt.float32
FP16 = mybir.dt.float16
FP8R = mybir.dt.float8e5
ALU = mybir.AluOpType
ACT = mybir.ActivationFunctionType
AX = mybir.AxisListType


def weight_units(q):
    return [("w", m, q, r) for m in range(3) for r in range(4)]


def first_steps():
    steps = [(u, None) for u in weight_units(0)]
    steps = [(u, (("a", "b")[n % 2], n // 2) if n < 8 else None) for n, (u, _) in enumerate(steps)]
    return steps + [(("y", i), None) for i in range(4)]


def batch_steps(weights, following):
    steps, n = [], 0
    for q in range(4):
        more = weight_units(q + 1) if weights and q < 3 else []
        for i in range(4):
            piece = None
            if following and n < 12 and n % 3 < 2:
                piece = (("a", "b")[n % 3], n // 3)
            steps.append((("h", q, i), piece))
            steps += [(u, None) for u in more[3 * i:3 * i + 3]]
            if following and q == 3 and i < 2:
                steps.append((("y", i), None))
            n += 1
    if following:
        steps += [(("y", 2), None), (("y", 3), None)]
    return steps


def adaln_ffn(nc, x, f, cond, w0, u0, gate_w, up_w, down_w, w1, u1, router_w, moe_a, moe_b, out):
    NB, T, C = x.shape
    P = 128
    KC = C // P
    NT = T // P
    I = gate_w.shape[0]
    NQ = I // 512
    NE, _, RANK = moe_a.shape
    BLK = 32
    NBLK = 512 // BLK
    assert (NT, KC, NQ, RANK) == (4, 4, 4, P)

    FP8_MAX = 448.0
    EPS = 1e-30
    E30 = float(np.exp(np.float32(30.0)))
    DOWN20 = 2.0 ** -20
    LEAST = 1.125 * 2.0 ** -6
    KY, KW, KH, KM = 8, 10, 10, 8

    PRO = first_steps()
    HEAD = batch_steps(True, True)
    MID = batch_steps(False, True)
    LAST = batch_steps(False, False)
    U_HEAD = len(PRO)
    U_MID = U_HEAD + len(HEAD)
    LM = len(MID)

    def units_before(b):
        return U_HEAD if isinstance(b, int) and b == 0 else (b - 1) * LM + U_MID

    x_t = x.rearrange("b (t p) c -> b p t c", p=P)
    f_t = f.rearrange("b (t p) c -> b p t c", p=P)
    out_t = out.rearrange("b (t p) c -> b p t c", p=P)
    x1_dram = nc.dram_tensor("x1_dram", [NB, P, NT, C], FP32, kind="Internal").ap()
    moe_a_v = moe_a.rearrange("e (k p) r -> p k e r", p=P)
    moe_b_v = moe_b.rearrange("e r c -> r e c")
    router_v = router_w.rearrange("(k p) e -> p k e", p=P)
    w_drams = (gate_w, up_w, down_w)

    ctx = ExitStack()
    with ctx:
        def sb(name, shape, dt=FP32):
            return ctx.enter_context(nc.sbuf_tensor(name, shape, dt))

        def sem(name):
            return ctx.enter_context(nc.semaphore(name))

        wg = sb("wg", [P, 2, KC, I], FP16)
        wu = sb("wu", [P, 2, KC, I], FP16)
        wd = sb("wd", [P, 2, I // P, C], FP16)
        f_nat = sb("f_nat", [P, NT, C])
        x_nat = sb("x_nat", [P, NT, C])
        x_res = sb("x_res", [P, NT, C])
        fT = sb("fT", [P, T])
        sig = sb("sig", [P, T])
        ek = sb("ek", [P, T])
        eu = sb("eu", [P, T])
        ekv = sb("ekv", [P, T])
        fwd_n = sb("fwd_n", [P, T])
        fwd_d = sb("fwd_d", [P, T])
        rd = sb("rd", [P, T])
        y_ch = sb("y_ch", [P, KC, T])
        yT = sb("yT", [P, 2, KC, T], FP16)
        hT = sb("hT", [P, 2, 2, KC, P], FP16)
        src = sb("src", [P, 4, 512])
        qp = sb("qp", [P, 2, 512])
        rc = sb("rc", [P, 2, 512], FP8R)
        rr = sb("rr", [P, 2, 512])
        qt = sb("qt", [P, 2, 512])
        deq = sb("deq", [P, 2, 512])
        silu = sb("silu", [P, 2, 512])
        amax = sb("amax", [P, 2, NBLK])
        scale = sb("scale", [P, 2, NBLK])
        rinv = sb("rinv", [P, 2, NBLK])
        nscale = sb("nscale", [P, 2, NBLK])
        ident = sb("ident", [P, P])
        cond_sb = sb("cond_sb", [P, NB, P])
        csum = sb("csum", [P, NB])
        tf = sb("tf", [P, NB])
        half = sb("half", [P, NB])
        ncb = sb("ncb", [P, NB])
        wv = sb("wv", [P, 2, KC])
        uv = sb("uv", [P, 2, KC])
        ew = sb("ew", [P, 2, KC])
        dw = sb("dw", [P, 2, KC])
        dec = sb("dec", [P, 2, KC, NB])
        kb = sb("kb", [P, 2, KC, NB])
        gb = sb("gb", [P, 2, KC, NB])
        tmp1 = sb("tmp1", [P, 2, KC, NB])
        tmp2 = sb("tmp2", [P, 2, KC, NB])
        ini = sb("ini", [P, 2])
        nleast = sb("nleast", [P, 1])
        gap = sb("gap", [P, 1])
        wa = wg[:, :, :, :].rearrange("p a k i -> p (a k i)")[:, 0:2 * KC * NE * RANK]\
            .rearrange("p (a k n) -> p a k n", a=2, k=KC)
        wb = wu[:, :, :, :].rearrange("p a k i -> p (a k i)")[:, 0:2 * NE * C]\
            .rearrange("p (a e n) -> p a e n", a=2, e=NE)
        raw = wd[:, :, :, :].rearrange("p a k i -> p (a k i)").bitcast(FP32)
        wa_raw = raw[:, 0:KC * NE * RANK].rearrange("p (k n) -> p k n", k=KC)
        wb_raw = raw[:, KC * NE * RANK:2 * KC * NE * RANK].rearrange("p (e n) -> p e n", e=NE)
        sq = src
        cbs = silu
        ms = qp
        mT = hT[:, :, :, :, :].rearrange("p s a k t -> p s a (k t)")
        rw = sb("rw", [P, KC, NE])
        ones = sb("ones", [P, 2])
        onehot = sb("onehot", [NE, NE, P])
        lower = sb("lower", [P, NE, NE])
        ssq = sb("ssq", [P, NT])
        nrm = sb("nrm", [P, NT])
        nr1 = sb("nr1", [P, NT])
        nr2 = sb("nr2", [P, NT])
        lg = sb("lg", [P, NT, NE])
        mx = sb("mx", [P, NT])
        pe_ = sb("pe_", [P, NT, NE])
        zz = sb("zz", [P, NT])
        gt = sb("gt", [P, NT, NE, NE])
        eq = sb("eq", [P, NT, NE, NE])
        cnt = sb("cnt", [P, NT, NE])
        cmb = sb("cmb", [P, NT, NE])
        cmbT = sb("cmbT", [NE, T])

        def bank(name):
            return ctx.enter_context(nc.psum_tensor(name, [P, 512], FP32))
        ps_gate, ps_up, ps_t, ps_m = bank("ps_gate"), bank("ps_up"), bank("ps_t"), bank("ps_m")
        ps_o = [bank(f"ps_o{i}") for i in range(NT)]

        s_const = sem("s_const")
        s_par = sem("s_par")
        s_csum = sem("s_csum")
        s_tf = sem("s_tf")
        s_prep = sem("s_prep")
        s_dw = sem("s_dw")
        s_wload = [sem(f"s_wload{i}") for i in range(4)]
        s_fnat = sem("s_fnat")
        s_xnat = sem("s_xnat")
        s_xres = sem("s_xres")
        s_x1out = sem("s_x1out")
        s_ftr = sem("s_ftr")
        s_xtr = sem("s_xtr")
        s_fT = sem("s_fT")
        s_sig = sem("s_sig")
        s_ek = sem("s_ek")
        s_eu = sem("s_eu")
        s_cd = sem("s_cd")
        s_ln = sem("s_ln")
        s_rd = sem("s_rd")
        s_nw = sem("s_nw")
        s_ytr = sem("s_ytr")
        s_ysrc = sem("s_ysrc")
        s_gate = sem("s_gate")
        s_up = sem("s_up")
        s_silu = sem("s_silu")
        s_h = sem("s_h")
        s_amax = sem("s_amax")
        s_scale = sem("s_scale")
        s_rinv = sem("s_rinv")
        s_nscale = sem("s_nscale")
        s_qp = sem("s_qp")
        s_rc = sem("s_rc")
        s_rr = sem("s_rr")
        s_qt = sem("s_qt")
        s_nq = sem("s_nq")
        s_deq = sem("s_deq")
        s_tr = sem("s_tr")
        s_hi = sem("s_hi")
        s_lo = sem("s_lo")
        s_down = sem("s_down")
        s_x1 = sem("s_x1")
        s_raw = sem("s_raw")
        s_rwl = sem("s_rwl")
        s_whi = sem("s_whi")
        s_wlo = sem("s_wlo")
        s_yhi = sem("s_yhi")
        s_ylo = sem("s_ylo")
        s_sq = sem("s_sq")
        s_lgt = sem("s_lgt")
        s_rt = sem("s_rt")
        s_rc2 = sem("s_rc2")
        s_sqrt = sem("s_sqrt")
        s_exp = sem("s_exp")
        s_ctr = sem("s_ctr")
        s_cT = sem("s_cT")
        s_cb = sem("s_cb")
        s_cbs = sem("s_cbs")
        s_e1 = sem("s_e1")
        s_m = sem("s_m")
        s_mhi = sem("s_mhi")
        s_mlo = sem("s_mlo")
        s_e2 = sem("s_e2")
        s_out = sem("s_out")
        s_outd = sem("s_outd")

        NCD = 15
        NRT = 16

        def part_of(unit, k, part):
            if unit[0] == "w":
                _, m, q, r = unit
                if m < 2:
                    at = P * (4 * q + r)
                    return (wg, wu)[m][:, part, :, at:at + P]
                return wd[:, part, 4 * q:4 * q + 4, P * r:P * r + P]
            if unit[0] == "y":
                return yT[:, part, :, P * unit[1]:P * unit[1] + P]
            n = 4 * unit[1] + unit[2]
            return hT[:, n % 2, part, :, :]

        power_of = {"w": KW, "y": KY, "h": KH}

        block = ctx.enter_context(nc.Block())

        @block.sync
        def _(sp):
            def load_weight(u, unit):
                _, m, q, r = unit
                if u >= 4:
                    sp.wait_ge(s_qp, u - 3)
                rows = w_drams[m][P * (4 * q + r):P * (4 * q + r + 1), :] if m < 2 else \
                    w_drams[m][P * r:P * (r + 1), 512 * q:512 * (q + 1)]
                sp.dma_start(src[:, u % 4, :], rows).then_inc(s_wload[u % 4], 16)

            def load_cond(j, b, source):
                if not (isinstance(j, int) and j == 0):
                    sp.wait_ge(s_ftr, j * KC)
                    sp.wait_ge(s_xtr, j * KC)
                sp.dma_start(f_nat[:, :, :], f_t[b]).then_inc(s_fnat, 16)
                sp.dma_start(x_nat[:, :, :], source[b]).then_inc(s_xnat, 16)

            def load_residual(j, b, source, done, value):
                if done is not None:
                    sp.wait_ge(done, value)
                sp.dma_start(x_res[:, :, :], source[b]).then_inc(s_xres, 16)

            sp.dma_start(cond_sb[:, :, :], cond.rearrange("(a b) d -> a b d", a=1).to_broadcast([P, NB, P]))\
                .then_inc(s_par, 16)
            for n, (w, u) in enumerate(((w0, u0), (w1, u1))):
                sp.dma_start(wv[:, n, :], w.rearrange("(k p) -> p k", p=P),
                             allow_slow_non_contiguous=True).then_inc(s_par, 16)
                sp.dma_start(uv[:, n, :], u.rearrange("(k p) -> p k", p=P),
                             allow_slow_non_contiguous=True).then_inc(s_par, 16)
            load_cond(0, 0, x_t)
            units = [unit for unit, _ in PRO + HEAD]
            for u in range(4):
                load_weight(u, units[u])
            load_residual(0, 0, x_t, None, 0)
            for u in range(4, U_MID):
                if u == U_HEAD:
                    load_cond(1, 1, x_t)
                if units[u][0] == "w":
                    load_weight(u, units[u])
            sp.dma_start(rw[:, :, :], router_v).then_inc(s_rwl, 16)

            def keep_x1(b):
                sp.wait_ge(s_x1, b * NT + NT)
                sp.dma_start(x1_dram[b], x_res[:, :, :]).then_inc(s_x1out, 16)

            keep_x1(0)
            load_residual(1, 1, x_t, s_x1out, 16)
            with sp.Fori(1, NB - 1) as b:
                load_cond(b + 1, b + 1, x_t)
                keep_x1(b)
                load_residual(b + 1, b + 1, x_t, s_x1out, b * 16 + 16)
            keep_x1(NB - 1)
            sp.wait_ge(s_down, 16 * NB)
            for k in range(KC):
                sp.dma_start(wa_raw[:, k, :].rearrange("p (e r) -> p e r", e=NE), moe_a_v[:, k, :, :])\
                    .then_inc(s_raw, 16)
            sp.dma_start(wb_raw, moe_b_v).then_inc(s_raw, 16)
            sp.wait_ge(s_x1out, 16 * NB)
            load_cond(NB, 0, x1_dram)
            load_residual(NB, 0, x1_dram, None, 0)

            def store_out(b):
                sp.wait_ge(s_out, b * NT + NT)
                sp.dma_start(out_t[b], x_res[:, :, :]).then_inc(s_outd, 16)

            with sp.Fori(0, NB - 1) as b:
                load_cond(b + (NB + 1), b + 1, x1_dram)
                store_out(b)
                load_residual(b, b + 1, x1_dram, s_outd, b * 16 + 16)
            store_out(NB - 1)
            sp.wait_ge(s_outd, 16 * NB)

        @block.gpsimd
        def _(pool):
            nc.gpsimd.memset(ident[:, :], 0.0).then_inc(s_const, 1)
            nc.gpsimd.memset(ones[:, :], 1.0).then_inc(s_const, 1)
            nc.gpsimd.memset(onehot[:, :, :], 0.0).then_inc(s_const, 1)
            nc.gpsimd.memset(lower[:, :, :], 1.0).then_inc(s_const, 1)
            pool.wait_ge(s_const, 4)
            nc.gpsimd.affine_select(out=ident[:, :], in_=ident[:, :], compare_op=ALU.not_equal, fill=1.0,
                                    base=0, pattern=[[-1, P]], channel_multiplier=1).then_inc(s_const, 1)
            nc.gpsimd.affine_select(out=onehot[:, :, :], in_=onehot[:, :, :], compare_op=ALU.not_equal, fill=1.0,
                                    base=0, pattern=[[-1, NE], [0, P]], channel_multiplier=1).then_inc(s_const, 1)
            nc.gpsimd.affine_select(out=lower[:, :, :], in_=lower[:, :, :], compare_op=ALU.is_gt, fill=0.0,
                                    base=0, pattern=[[1, NE], [-1, NE]], channel_multiplier=0).then_inc(s_const, 1)

            def blocks(ap):
                return ap.rearrange("p (n k) -> p n k", k=BLK)

            def spread(ap):
                return ap.unsqueeze(2).to_broadcast([P, NBLK, BLK])

            def normalise(u, k, unit):
                pool.wait_ge(s_rinv, u + 1)
                if not (isinstance(u, int) and u < 2):
                    pool.wait_ge(s_qt, u - 1)
                nc.gpsimd.tensor_tensor(blocks(qp[:, k % 2, :]), blocks(src[:, k % 4, :]),
                                        spread(rinv[:, k % 2, :]), ALU.mult).then_inc(s_qp, 1)

            def dequantise(u, k):
                pool.wait_ge(s_nq, u + 1)
                pool.wait_ge(s_nscale, u + 1)
                if not (isinstance(u, int) and u < 2):
                    pool.wait_ge(s_tr, u - 1)
                nc.gpsimd.tensor_tensor(blocks(deq[:, k % 2, :]), blocks(qt[:, k % 2, :]),
                                        spread(nscale[:, k % 2, :]), ALU.mult).then_inc(s_deq, 1)

            def run(steps, base, k0):
                for k, (unit, _) in enumerate(steps):
                    if k0 + k > 0:
                        dequantise(base + (k - 1), k0 + k - 1)
                    normalise(base + k, k0 + k, unit)

            run(PRO, 0, 0)
            run(HEAD, U_HEAD, U_HEAD)
            with pool.Fori(1, NB - 1) as b:
                run(MID, units_before(b), U_MID)
            run(LAST, units_before(NB - 1), U_MID)
            dequantise(units_before(NB - 1) + 15, U_MID + 15)

            def squares(b):
                pool.wait_ge(s_cd, (b + NB + 1) * KC * NCD)
                if not (isinstance(b, int) and b == 0):
                    pool.wait_ge(s_lgt, b)
                nc.gpsimd.tensor_tensor(sq[:, :, :], y_ch[:, :, :], y_ch[:, :, :], ALU.mult).then_inc(s_sq, 1)

            squares(0)
            with pool.Fori(1, NB) as b:
                squares(b)

        @block.scalar
        def _(act):
            act.wait_ge(s_csum, 1)
            nc.scalar.activation(tf[:, :], csum[:, :], ACT.Sigmoid).then_inc(s_tf, 1)
            act.wait_ge(s_par, 5 * 16)
            nc.scalar.activation(ew[:, :, :], wv[:, :, :], ACT.Exp).then_inc(s_dw, 1)
            act.wait_ge(s_dw, 1)
            nc.scalar.activation(dw[:, :, :], ew[:, :, :], ACT.Exp, scale=-1.0).then_inc(s_dw, 1)

            def cond_a(layer, j, c):
                act.wait_ge(s_ftr, j + 1)
                if not (isinstance(j, int) and j == 0):
                    act.wait_ge(s_cd, j * NCD)
                nc.scalar.activation(fT[:, :], ps_m[:, :], ACT.Copy).then_inc(s_fT, 1)
                act.wait_ge(s_fT, j + 1)
                nc.scalar.activation(ek[:, :], fT[:, :], ACT.Exp).then_inc(s_ek, 1)
                nc.scalar.activation(eu[:, :], fT[:, :], ACT.Exp, bias=uv[:, layer, c:c + 1]).then_inc(s_eu, 1)
                act.wait_ge(s_xtr, j + 1)
                nc.scalar.activation(sig[:, :], ps_m[:, :], ACT.Sigmoid).then_inc(s_sig, 1)

            def cond_ln(j):
                act.wait_ge(s_cd, j * NCD + 12)
                nc.scalar.activation(rd[:, :], ek[:, :], ACT.Ln).then_inc(s_ln, 1)
                act.wait_ge(s_ln, j + 1)
                nc.scalar.activation(rd[:, :], rd[:, :], ACT.Exp, scale=-1.0).then_inc(s_rd, 1)

            def high(u, k, unit, h_at, g0):
                act.wait_ge(s_tr, u + 1)
                dst = part_of(unit, k, 0)
                if unit[0] == "h":
                    n = 4 * unit[1] + unit[2]
                    if not (isinstance(g0, int) and g0 + n < 2):
                        act.wait_ge(s_down, g0 + n - 1)
                if unit[0] == "y" and h_at is not None:
                    act.wait_ge(s_up, h_at + 13 + unit[1])
                nc.scalar.activation(dst, ps_t[:, :].rearrange("p (k t) -> p k t", k=4), ACT.Copy)\
                    .then_inc(s_hi, 1)

            def carry(u):
                if not isinstance(u, int):
                    nc.scalar.activation(gap[:, 0:1], nleast[:, 0:1], ACT.Copy)

            def round_constant(u, k):
                act.wait_ge(s_qp, u + 1)
                carry(u)
                nc.scalar.activation(rc[:, k % 2, :], qp[:, k % 2, :], ACT.Abs, scale=0.9375 / DOWN20,
                                     saturate=False)\
                    .then_inc(s_rc, 1)
                act.wait_ge(s_rc, u + 1)
                if not (isinstance(u, int) and u < 2):
                    act.wait_ge(s_nq, u - 1)
                carry(u)
                nc.scalar.activation(rr[:, k % 2, :], rc[:, k % 2, :], ACT.Relu, scale=1.125, bias=nleast[:, 0:1])\
                    .then_inc(s_rr, 1)

            def own(u, k, unit, g0, y0):
                if unit[0] == "h":
                    n = 4 * unit[1] + unit[2]
                    act.wait_ge(s_gate, g0 + n + 1)
                    if not (isinstance(g0, int) and g0 + n < 2):
                        act.wait_ge(s_h, g0 + n - 1)
                    nc.scalar.activation(silu[:, n % 2, :], ps_gate[:, :], ACT.Silu, scale=2.0 ** -(KY + KW))\
                        .then_inc(s_silu, 1)
                if unit[0] == "y":
                    act.wait_ge(s_ytr, y0 + unit[1] + 1)
                    act.wait_ge(s_qp, u - 3)
                    nc.scalar.activation(src[:, k % 4, :], ps_m[:, :], ACT.Copy).then_inc(s_ysrc, 1)

            def run(steps, base, k0, before, g0, y0, j0, h_at):
                units = before + [unit for unit, _ in steps]
                nb = len(before)
                for k, (unit, piece) in enumerate(steps):
                    if k0 + k >= 2:
                        high(base + (k - 2), k0 + k - 2, units[nb + k - 2], h_at if k >= 2 else None, g0)
                    if k0 + k >= 1:
                        round_constant(base + (k - 1), k0 + k - 1)
                    own(base + k, k0 + k, unit, g0, y0)
                    if piece and piece[0] == "a":
                        cond_a(0, j0 + piece[1], piece[1])
                    if piece and piece[0] == "b":
                        cond_ln(j0 + piece[1])

            tail = [("y", 2), ("y", 3)]
            run(PRO, 0, 0, [], 0, 0, 0, None)
            run(HEAD, U_HEAD, U_HEAD, tail, 0, 4, 4, 0)
            with act.Fori(1, NB - 1) as b:
                run(MID, units_before(b), U_MID, tail, b * 16, b * 4 + 4, b * 4 + 4, b * 16)
            uL, gL = units_before(NB - 1), 16 * (NB - 1)
            run(LAST, uL, U_MID, tail, gL, 4 * NB, 4 * NB, gL)
            high(uL + 14, U_MID + 14, ("h", 3, 2), None, gL)
            round_constant(uL + 15, U_MID + 15)
            high(uL + 15, U_MID + 15, ("h", 3, 3), None, gL)

            act.wait_ge(s_raw, 5 * 16)
            nc.scalar.activation(wa[:, 0, :, :], wa_raw, ACT.Copy, scale=2.0 ** KM).then_inc(s_whi, 1)
            nc.scalar.activation(wb[:, 0, :, :], wb_raw, ACT.Copy, scale=2.0 ** KM).then_inc(s_whi, 1)

            def y_high(b):
                act.wait_ge(s_cd, (b + NB + 1) * KC * NCD)
                if not (isinstance(b, int) and b == 0):
                    act.wait_ge(s_e1, b * NE)
                nc.scalar.activation(yT[:, 0, :, :], y_ch[:, :, :], ACT.Copy, scale=2.0 ** KM).then_inc(s_yhi, 1)

            def router(b):
                act.wait_ge(s_rt, b * NRT + 1)
                nc.scalar.activation(nrm[:, :], ssq[:, :], ACT.Sqrt).then_inc(s_sqrt, 1)
                act.wait_ge(s_rt, b * NRT + 8)
                nc.scalar.activation(pe_[:, :, :], lg[:, :, :], ACT.Exp).then_inc(s_exp, 1)
                act.wait_ge(s_ctr, b + 1)
                nc.scalar.activation(cmbT[:, :], ps_t[0:NE, :], ACT.Copy).then_inc(s_cT, 1)

            def expert_a(b, e):
                act.wait_ge(s_cb, b * NE + (e + 1))
                if e >= 2 or not (isinstance(b, int) and b == 0):
                    act.wait_ge(s_m, b * NE + (e - 1))
                nc.scalar.activation(cbs[:, e % 2, :], ps_t[:, :], ACT.Copy).then_inc(s_cbs, 1)

            def expert_b(b, e):
                act.wait_ge(s_m, b * NE + (e + 1))
                if e >= 2 or not (isinstance(b, int) and b == 0):
                    act.wait_ge(s_e2, b * NE + (e - 1))
                nc.scalar.activation(mT[:, e % 2, 0, :], ms[:, e % 2, :], ACT.Copy).then_inc(s_mhi, 1)

            def experts(b, following):
                for e in range(NE + 1):
                    if e < NE:
                        expert_a(b, e)
                    if e > 0:
                        expert_b(b, e - 1)
                    if following and e < NE:
                        j = (b + (NB + 1)) * KC + e // 2
                        if e % 2 == 0:
                            cond_a(1, j, e // 2)
                        else:
                            cond_ln(j)

            for c in range(KC):
                cond_a(1, NB * KC + c, c)
                cond_ln(NB * KC + c)
            y_high(0)
            router(0)
            experts(0, True)
            with act.Fori(1, NB - 1) as b:
                y_high(b)
                router(b)
                experts(b, True)
            y_high(NB - 1)
            router(NB - 1)
            experts(NB - 1, False)

        @block.vector
        def _(dve):
            v = nc.vector
            n = [0]

            def link(ins):
                n[0] += 1
                ins.then_inc(s_prep, 1)
                dve.wait_ge(s_prep, n[0])

            v.memset(nleast[:, :], -LEAST).then_inc(s_prep, 1)
            n[0] += 1
            dve.wait_ge(s_par, 5 * 16)
            v.tensor_reduce(csum[:, :], cond_sb[:, :, :], AX.X, ALU.add).then_inc(s_csum, 1)
            dve.wait_ge(s_tf, 1)
            link(v.tensor_scalar(half[:, :], tf[:, :], 0.5, 0.5, ALU.mult, ALU.add))
            link(v.tensor_scalar(ncb[:, :], tf[:, :], -0.2, -0.8, ALU.mult, ALU.add))
            dve.wait_ge(s_dw, 2)
            for layer in range(2):
                link(v.tensor_tensor(dec[:, layer], dw[:, layer].unsqueeze(2).to_broadcast([P, KC, NB]),
                                     half[:, :].unsqueeze(1).to_broadcast([P, KC, NB]), ALU.mult))
            link(v.tensor_scalar(tmp1[:, :, :, :], dec[:, :, :, :], -1.0, 1.0, ALU.mult, ALU.add))
            link(v.tensor_scalar(tmp2[:, :, :, :], dec[:, :, :, :], 1.0, None, ALU.add))
            link(v.tensor_tensor(tmp1[:, :, :, :], tmp1[:, :, :, :], tmp2[:, :, :, :], ALU.mult))
            link(v.tensor_scalar(kb[:, :, :, :], tmp1[:, :, :, :], 1e-12, None, ALU.max))
            link(v.reciprocal(tmp2[:, :, :, :], kb[:, :, :, :]))
            link(v.tensor_tensor(gb[:, :, :, :], dec[:, :, :, :], tmp2[:, :, :, :], ALU.mult))

            def cond_a(layer, j, c, b):
                at = j * NCD
                d = dec[:, layer, c, bass.ds(b, 1)]
                dd = d.to_broadcast([P, T])

                def did(ins):
                    ins.then_inc(s_cd, 1)
                dve.wait_ge(s_ek, j + 1)
                did(v.scalar_tensor_tensor(out=ekv[:, :], in0=ek[:, :], scalar=E30, in1=fT[:, :],
                                           op0=ALU.min, op1=ALU.mult))
                did(v.tensor_scalar(ek[:, :], ek[:, :], E30, None, ALU.min))
                dve.wait_ge(s_cd, at + 1)
                did(v.tensor_tensor_scan(fwd_n[:, :], dd, ekv[:, :], 0.0, ALU.mult, ALU.add))
                dve.wait_ge(s_cd, at + 2)
                did(v.tensor_tensor_scan(fwd_d[:, :], dd, ek[:, :], 0.0, ALU.mult, ALU.add))
                dve.wait_ge(s_cd, at + 3)
                g = gb[:, layer, c, bass.ds(b, 1)]
                did(v.tensor_tensor(ini[:, 0:1], fwd_n[:, T - 1:T], g, ALU.mult))
                dve.wait_ge(s_cd, at + 4)
                did(v.tensor_tensor(ini[:, 1:2], fwd_d[:, T - 1:T], g, ALU.mult))
                dve.wait_ge(s_cd, at + 5)
                did(v.tensor_tensor_scan(ekv[:, ::-1], dd, fwd_n[:, ::-1], ini[:, 0:1], ALU.mult, ALU.add))
                dve.wait_ge(s_cd, at + 6)
                did(v.tensor_tensor_scan(ek[:, ::-1], dd, fwd_d[:, ::-1], ini[:, 1:2], ALU.mult, ALU.add))
                dve.wait_ge(s_eu, j + 1)
                dve.wait_ge(s_cd, at + 8)
                k = kb[:, layer, c, bass.ds(b, 1)]
                did(v.tensor_scalar(eu[:, :], eu[:, :], E30, None, ALU.min))
                dve.wait_ge(s_cd, at + 9)
                did(v.tensor_tensor(fwd_n[:, :], eu[:, :], fT[:, :], ALU.mult))
                did(v.scalar_tensor_tensor(out=fwd_d[:, :], in0=ek[:, :], scalar=k, in1=eu[:, :],
                                           op0=ALU.mult, op1=ALU.add))
                dve.wait_ge(s_cd, at + 11)
                did(v.tensor_scalar(ek[:, :], fwd_d[:, :], 1e-8, None, ALU.max))
                did(v.scalar_tensor_tensor(out=fwd_n[:, :], in0=ekv[:, :], scalar=k, in1=fwd_n[:, :],
                                           op0=ALU.mult, op1=ALU.add))

            def cond_b(layer, j, c, b, y_free):
                at = j * NCD
                dve.wait_ge(s_rd, j + 1)
                v.tensor_tensor(fwd_d[:, :], ek[:, :], rd[:, :], ALU.mult).then_inc(s_nw, 1)
                dve.wait_ge(s_nw, j * 3 + 1)
                v.scalar_tensor_tensor(out=fwd_d[:, :], in0=fwd_d[:, :], scalar=2.0, in1=rd[:, :],
                                       op0=ALU.subtract, op1=ALU.mult).then_inc(s_nw, 1)
                dve.wait_ge(s_sig, j + 1)
                dve.wait_ge(s_cd, at + 13)
                v.scalar_tensor_tensor(out=fwd_n[:, :], in0=fwd_n[:, :], scalar=ncb[:, bass.ds(b, 1)],
                                       in1=sig[:, :], op0=ALU.mult, op1=ALU.mult).then_inc(s_nw, 1)
                dve.wait_ge(s_nw, j * 3 + 3)
                if c == 0:
                    y_free()
                v.tensor_tensor(y_ch[:, c, :], fwd_n[:, :], fwd_d[:, :], ALU.mult).then_inc(s_cd, 2)

            def blocks(ap):
                return ap.rearrange("p (n k) -> p n k", k=BLK)

            def low(u, k, unit):
                dve.wait_ge(s_hi, u + 1)
                v.tensor_tensor(part_of(unit, k, 1), ps_t[:, :].rearrange("p (k t) -> p k t", k=4),
                                part_of(unit, k, 0), ALU.subtract).then_inc(s_lo, 1)

            def rounded(u, k):
                dve.wait_ge(s_rr, u + 1)
                if not (isinstance(u, int) and u < 2):
                    dve.wait_ge(s_deq, u - 1)
                v.scalar_tensor_tensor(out=qt[:, k % 2, :], in0=rr[:, k % 2, :], scalar=LEAST,
                                       in1=qp[:, k % 2, :], op0=ALU.add, op1=ALU.add).then_inc(s_qt, 1)
                dve.wait_ge(s_qt, u + 1)
                v.scalar_tensor_tensor(out=qt[:, k % 2, :], in0=rr[:, k % 2, :], scalar=LEAST,
                                       in1=qt[:, k % 2, :], op0=ALU.add, op1=ALU.subtract).then_inc(s_nq, 1)

            def scales(u, k, unit, g0, y0, loads):
                if unit[0] == "h":
                    m = 4 * unit[1] + unit[2]
                    dve.wait_ge(s_silu, g0 + m + 1)
                    dve.wait_ge(s_up, g0 + m + 1)
                    dve.wait_ge(s_qp, u - 3)
                    v.scalar_tensor_tensor(out=src[:, k % 4, :], in0=ps_up[:, :], scalar=2.0 ** -(KY + KW),
                                           in1=silu[:, m % 2, :], op0=ALU.mult, op1=ALU.mult).then_inc(s_h, 1)
                    dve.wait_ge(s_h, g0 + m + 1)
                elif unit[0] == "y":
                    dve.wait_ge(s_ysrc, y0 + unit[1] + 1)
                else:
                    loads[k % 4] += 16
                    dve.wait_ge(s_wload[k % 4], loads[k % 4])
                v.tensor_reduce(amax[:, k % 2, :], blocks(src[:, k % 4, :]), AX.X, ALU.max,
                                apply_absolute_value=True).then_inc(s_amax, 1)
                dve.wait_ge(s_amax, u + 1)
                v.tensor_scalar(scale[:, k % 2, :], amax[:, k % 2, :], 1.0 / (FP8_MAX * DOWN20), EPS / DOWN20,
                                ALU.mult, ALU.max).then_inc(s_scale, 1)
                dve.wait_ge(s_scale, u + 1)
                if not (isinstance(u, int) and u < 2):
                    dve.wait_ge(s_qp, u - 1)
                v.reciprocal(rinv[:, k % 2, :], scale[:, k % 2, :]).then_inc(s_rinv, 1)
                if not (isinstance(u, int) and u < 2):
                    dve.wait_ge(s_deq, u - 1)
                v.tensor_scalar(nscale[:, k % 2, :], scale[:, k % 2, :], -(2.0 ** power_of[unit[0]]), None,
                                ALU.mult).then_inc(s_nscale, 1)

            def sum_x1(b, i):
                dve.wait_ge(s_down, b * 16 + (13 + i))
                if i == 0:
                    dve.wait_ge(s_xres, b * 16 + 16)
                v.scalar_tensor_tensor(out=x_res[:, i, :], in0=ps_o[i][:, :], scalar=2.0 ** -(KH + KW),
                                       in1=x_res[:, i, :], op0=ALU.mult, op1=ALU.add).then_inc(s_x1, 1)

            def run(steps, base, k0, before, g0, y0, j0, b, loads):
                units = before + [unit for unit, _ in steps]
                nb = len(before)
                for k, (unit, piece) in enumerate(steps):
                    if k0 + k >= 2:
                        low(base + (k - 2), k0 + k - 2, units[nb + k - 2])
                    if k0 + k >= 1:
                        rounded(base + (k - 1), k0 + k - 1)
                    scales(base + k, k0 + k, unit, g0, y0, loads)
                    if piece and piece[0] == "a":
                        cond_a(0, j0 + piece[1], piece[1], b)
                    if piece and piece[0] == "b":
                        cond_b(0, j0 + piece[1], piece[1], b,
                               (lambda: None) if isinstance(y0, int) and y0 == 0
                               else (lambda: dve.wait_ge(s_ytr, y0)))

            tail = [("y", 2), ("y", 3)]
            loads = [0] * 4
            run(PRO, 0, 0, [], 0, 0, 0, 0, loads)
            run(HEAD, U_HEAD, U_HEAD, tail, 0, 4, 4, 1, loads)
            for i in range(NT):
                sum_x1(0, i)
            with dve.Fori(1, NB - 1) as b:
                run(MID, units_before(b), U_MID, tail, b * 16, b * 4 + 4, b * 4 + 4, b + 1, loads)
                for i in range(NT):
                    sum_x1(b, i)
            uL, gL = units_before(NB - 1), 16 * (NB - 1)
            run(LAST, uL, U_MID, tail, gL, 4 * NB, 4 * NB, 0, loads)
            low(uL + 14, U_MID + 14, ("h", 3, 2))
            rounded(uL + 15, U_MID + 15)
            low(uL + 15, U_MID + 15, ("h", 3, 3))
            for i in range(NT):
                sum_x1(NB - 1, i)

            dve.wait_ge(s_whi, 1)
            v.scalar_tensor_tensor(out=wa[:, 1, :, :], in0=wa_raw, scalar=2.0 ** KM, in1=wa[:, 0, :, :],
                                   op0=ALU.mult, op1=ALU.subtract).then_inc(s_wlo, 1)
            dve.wait_ge(s_whi, 2)
            v.scalar_tensor_tensor(out=wb[:, 1, :, :], in0=wb_raw, scalar=2.0 ** KM, in1=wb[:, 0, :, :],
                                   op0=ALU.mult, op1=ALU.subtract).then_inc(s_wlo, 1)

            def y_low(b):
                dve.wait_ge(s_yhi, b + 1)
                v.scalar_tensor_tensor(out=yT[:, 1, :, :].rearrange("p k t -> p (k t)"),
                                       in0=y_ch[:, :, :].rearrange("p k t -> p (k t)"), scalar=2.0 ** KM,
                                       in1=yT[:, 0, :, :].rearrange("p k t -> p (k t)"),
                                       op0=ALU.mult, op1=ALU.subtract).then_inc(s_ylo, 1)

            def router(b):
                at = b * NRT
                m = [0]

                def did(ins):
                    m[0] += 1
                    ins.then_inc(s_rt, 1)
                    dve.wait_ge(s_rt, at + m[0])
                over_e = [P, NT, NE]
                dve.wait_ge(s_lgt, b + 1)
                lgs = ps_gate[:, 0:NT * 16].rearrange("p (i n) -> p i n", n=16)
                did(v.tensor_scalar(ssq[:, :], lgs[:, :, NE], 1e-24, None, ALU.max))
                dve.wait_ge(s_sqrt, b + 1)
                did(v.reciprocal(nr1[:, :], nrm[:, :]))
                did(v.tensor_tensor(nr1[:, :], nr1[:, :], ssq[:, :], ALU.mult))
                did(v.tensor_tensor(nr1[:, :], nr1[:, :], nrm[:, :], ALU.add))
                did(v.reciprocal(nr2[:, :], nr1[:, :]))
                did(v.scalar_tensor_tensor(out=lg[:, :, :], in0=lgs[:, :, 0:NE], scalar=2.0,
                                           in1=nr2[:, :].unsqueeze(2).to_broadcast(over_e),
                                           op0=ALU.mult, op1=ALU.mult))
                did(v.tensor_reduce(mx[:, :], lg[:, :, :], AX.X, ALU.max))
                did(v.tensor_tensor(lg[:, :, :], lg[:, :, :], mx[:, :].unsqueeze(2).to_broadcast(over_e),
                                    ALU.subtract))
                dve.wait_ge(s_exp, b + 1)
                did(v.tensor_reduce(zz[:, :], pe_[:, :, :], AX.X, ALU.add))
                did(v.reciprocal(mx[:, :], zz[:, :]))
                did(v.tensor_tensor(pe_[:, :, :], pe_[:, :, :], mx[:, :].unsqueeze(2).to_broadcast(over_e),
                                    ALU.mult))
                mine = pe_[:, :, :].unsqueeze(3).to_broadcast([P, NT, NE, NE])
                theirs = pe_[:, :, :].unsqueeze(2).to_broadcast([P, NT, NE, NE])
                v.tensor_tensor(gt[:, :, :, :], theirs, mine, ALU.is_gt).then_inc(s_rc2, 1)
                v.tensor_tensor(eq[:, :, :, :], theirs, mine, ALU.is_equal).then_inc(s_rc2, 1)
                dve.wait_ge(s_rc2, b * 4 + 2)
                v.tensor_tensor(eq[:, :, :, :], eq[:, :, :, :],
                                lower[:, :, :].unsqueeze(1).to_broadcast([P, NT, NE, NE]), ALU.mult)\
                    .then_inc(s_rc2, 1)
                dve.wait_ge(s_rc2, b * 4 + 3)
                v.tensor_tensor(gt[:, :, :, :], gt[:, :, :, :], eq[:, :, :, :], ALU.add).then_inc(s_rc2, 1)
                dve.wait_ge(s_rc2, b * 4 + 4)
                did(v.tensor_reduce(cnt[:, :, :], gt[:, :, :, :], AX.X, ALU.add))
                did(v.scalar_tensor_tensor(out=cmb[:, :, :], in0=cnt[:, :, :], scalar=1.5, in1=pe_[:, :, :],
                                           op0=ALU.is_lt, op1=ALU.mult))
                did(v.tensor_reduce(zz[:, :], cmb[:, :, :], AX.X, ALU.add))
                did(v.reciprocal(mx[:, :], zz[:, :]))
                did(v.tensor_tensor(cmb[:, :, :], cmb[:, :, :], mx[:, :].unsqueeze(2).to_broadcast(over_e),
                                    ALU.mult))
                assert m[0] == NRT

            ps_e = (ps_gate, ps_up)

            def expert_a(b, e):
                dve.wait_ge(s_e1, b * NE + (e + 1))
                dve.wait_ge(s_cbs, b * NE + (e + 1))
                if e >= 2 or not (isinstance(b, int) and b == 0):
                    dve.wait_ge(s_mhi, b * NE + (e - 1))
                v.scalar_tensor_tensor(out=ms[:, e % 2, :], in0=ps_e[e % 2][:, :], scalar=2.0 ** -KM,
                                       in1=cbs[:, e % 2, :], op0=ALU.mult, op1=ALU.mult).then_inc(s_m, 1)

            def expert_b(b, e):
                dve.wait_ge(s_mhi, b * NE + (e + 1))
                v.tensor_tensor(mT[:, e % 2, 1, :], ms[:, e % 2, :], mT[:, e % 2, 0, :], ALU.subtract)\
                    .then_inc(s_mlo, 1)

            def finish(b):
                for i in range(NT):
                    dve.wait_ge(s_e2, b * NE + NE)
                    dve.wait_ge(s_xres, (b + NB) * 16 + 16)
                    v.scalar_tensor_tensor(out=x_res[:, i, :], in0=ps_o[i][:, :], scalar=2.0 ** -(2 * KM),
                                           in1=x_res[:, i, :], op0=ALU.mult, op1=ALU.add).then_inc(s_out, 1)

            def y_used(b):
                def wait():
                    dve.wait_ge(s_lgt, b + 1)
                    dve.wait_ge(s_ylo, b + 1)
                    dve.wait_ge(s_sq, b + 1)
                return wait

            def experts(b, following):
                for e in range(NE + 1):
                    if e < NE:
                        expert_a(b, e)
                    if e > 0:
                        expert_b(b, e - 1)
                    if following and e < NE:
                        j = (b + (NB + 1)) * KC + e // 2
                        if e % 2 == 0:
                            cond_a(1, j, e // 2, b + 1)
                        else:
                            cond_b(1, j, e // 2, b + 1, y_used(b))
                finish(b)

            for c in range(KC):
                cond_a(1, NB * KC + c, c, 0)
                cond_b(1, NB * KC + c, c, 0, lambda: dve.wait_ge(s_ytr, 4 * NB))
            y_low(0)
            router(0)
            experts(0, True)
            with dve.Fori(1, NB - 1) as b:
                y_low(b)
                router(b)
                experts(b, True)
            y_low(NB - 1)
            router(NB - 1)
            experts(NB - 1, False)

        @block.tensor
        def _(pe):
            t = nc.tensor
            pe.wait_ge(s_const, 7)

            def split_product(bank_, lhs, rhs, nk, first, last, done=None):
                for k in range(nk):
                    for n, (a, c) in enumerate(((0, 0), (0, 1), (1, 0))):
                        ins = t.matmul(bank_, lhs(a, k), rhs(c, k), start=first and k == 0 and n == 0,
                                       stop=last and k == nk - 1 and n == 2)
                if done is not None:
                    ins.then_inc(done, 1)

            def transpose4(bank_, tiles, done):
                for i, tile in enumerate(tiles):
                    ins = t.transpose(bank_[:, P * i:P * i + P], tile, ident[:, :])
                ins.then_inc(done, 1)

            def cond_a(j, c, bank_free):
                if c == 0:
                    pe.wait_ge(s_fnat, (j // KC) * 16 + 16 if isinstance(j, int) else j * 4 + 16)
                    pe.wait_ge(s_xnat, (j // KC) * 16 + 16 if isinstance(j, int) else j * 4 + 16)
                bank_free(j)
                transpose4(ps_m, [f_nat[:, i, P * c:P * c + P] for i in range(NT)], s_ftr)
                pe.wait_ge(s_fT, j + 1)
                transpose4(ps_m, [x_nat[:, i, P * c:P * c + P] for i in range(NT)], s_xtr)

            def gate_up(g, q, i):
                lhs = lambda a, k: yT[:, a, k, P * i:P * i + P]
                if not (isinstance(g, int) and g == 0):
                    pe.wait_ge(s_silu, g)
                split_product(ps_gate[:, :], lhs, lambda c, k: wg[:, c, k, 512 * q:512 * q + 512], KC, True, True,
                              s_gate)
                if not (isinstance(g, int) and g == 0):
                    pe.wait_ge(s_h, g)
                split_product(ps_up[:, :], lhs, lambda c, k: wu[:, c, k, 512 * q:512 * q + 512], KC, True, True,
                              s_up)

            def down(u, g, q, i, b):
                pe.wait_ge(s_lo, u + 1)
                if q == 0 and not (isinstance(b, int) and b == 0):
                    pe.wait_ge(s_x1, (b - 1) * NT + (i + 1))
                n = (4 * q + i) % 2
                split_product(ps_o[i][:, :], lambda a, k: hT[:, n, a, k, :], lambda c, k: wd[:, c, 4 * q + k, :],
                              4, q == 0, q == NQ - 1, s_down)

            def ready_y(base, i):
                return base - (6, 4, 1, 0)[i]

            def parts(u):
                pe.wait_ge(s_deq, u + 1)
                if not (isinstance(u, int) and u == 0):
                    pe.wait_ge(s_lo, u)
                k = parts.k
                transpose4(ps_t, [deq[:, k % 2, P * n:P * n + P] for n in range(4)], s_tr)

            def run(steps, base, k0, before, g0, y0, j0, b, ready):
                units = before + [unit for unit, _ in steps]
                nb = len(before)
                for k, (unit, piece) in enumerate(steps):
                    if unit[0] == "h":
                        _, q, i = unit
                        if b is not None and isinstance(b, int) and b == 0:
                            pe.wait_ge(s_lo, ready[unit])
                        elif q == 0:
                            pe.wait_ge(s_lo, ready_y(base, i))
                        gate_up(g0 + (4 * q + i), q, i)
                    if unit[0] == "y":
                        i = unit[1]
                        if i == 0:
                            pe.wait_ge(s_cd, (j0 + KC) * NCD)
                            pe.wait_ge(s_sig, j0 + KC)
                        else:
                            pe.wait_ge(s_ysrc, y0 + i)
                        transpose4(ps_m, [y_ch[:, c, P * i:P * i + P] for c in range(KC)], s_ytr)
                    if k0 + k >= 1:
                        parts.k = k0 + k - 1
                        parts(base + (k - 1))
                    if k0 + k >= 2:
                        past = units[nb + k - 2]
                        if past[0] == "h":
                            down(base + (k - 2), None, past[1], past[2], b)
                    if piece and piece[0] == "a":
                        j = j0 + piece[1]

                        def free(j, c=piece[1]):
                            if c > 0:
                                pe.wait_ge(s_sig, j)
                            elif not (isinstance(y0, int) and y0 == 0):
                                pe.wait_ge(s_ysrc, y0)
                        cond_a(j, piece[1], free)

            order = {unit: n for n, (unit, _) in enumerate(PRO + HEAD) if unit[0] == "w"}
            ready = {}
            for unit, _ in HEAD:
                if unit[0] == "h":
                    _, q, i = unit
                    need = max(order[("w", m, q, r)] for m in range(2) for r in range(4)) + 1
                    ready[unit] = max(need, U_HEAD - 3 + i)
            order_d = {q: max(order[("w", 2, q, r)] for r in range(4)) + 1 for q in range(NQ)}
            for n, (unit, _) in enumerate(HEAD):
                if unit[0] == "h":
                    assert order_d[unit[1]] <= U_HEAD + n + 1
                    assert ready[unit] <= U_HEAD + n - 1 or n < 2

            tail = [("y", 2), ("y", 3)]
            run(PRO, 0, 0, [], 0, 0, 0, 0, None)
            run_head = HEAD
            run(run_head, U_HEAD, U_HEAD, tail, 0, 4, 4, 0, ready)
            with pe.Fori(1, NB - 1) as b:
                run(MID, units_before(b), U_MID, tail, b * 16, b * 4 + 4, b * 4 + 4, b, None)
            uL, gL = units_before(NB - 1), 16 * (NB - 1)
            run(LAST, uL, U_MID, tail, gL, 4 * NB, 4 * NB, NB - 1, None)
            down(uL + 14, None, 3, 2, NB - 1)
            parts.k = U_MID + 15
            parts(uL + 15)
            down(uL + 15, None, 3, 3, NB - 1)

            ps_e = (ps_gate, ps_up)

            def router(b):
                pe.wait_ge(s_rwl, 16)
                pe.wait_ge(s_cd, (b + (NB + 1)) * KC * NCD)
                pe.wait_ge(s_sq, b + 1)
                if isinstance(b, int) and b == 0:
                    pe.wait_ge(s_h, 16 * NB)
                else:
                    pe.wait_ge(s_m, b * NE)
                for i in range(NT):
                    for k in range(KC):
                        t.matmul(ps_gate[:, 16 * i:16 * i + NE], y_ch[:, k, P * i:P * i + P], rw[:, k, :],
                                 start=k == 0, stop=k == KC - 1)
                    for k in range(KC):
                        ins = t.matmul(ps_gate[:, 16 * i + NE:16 * i + NE + 2], sq[:, k, P * i:P * i + P], ones[:, :],
                                       start=k == 0, stop=k == KC - 1)
                ins.then_inc(s_lgt, 1)

            def combine(b):
                pe.wait_ge(s_rt, b * NRT + NRT)
                if isinstance(b, int) and b == 0:
                    pe.wait_ge(s_lo, uL + 16)
                else:
                    pe.wait_ge(s_cbs, b * NE)
                for i in range(NT):
                    ins = t.transpose(ps_t[0:NE, P * i:P * i + P], cmb[:, i, :], ident[:, :])
                ins.then_inc(s_ctr, 1)

            def spread(b, e):
                if e == 0:
                    pe.wait_ge(s_cT, b + 1)
                else:
                    pe.wait_ge(s_cbs, b * NE + e)
                t.matmul(ps_t[:, :], onehot[:, e, :], cmbT[:, :], start=True, stop=True).then_inc(s_cb, 1)

            def first(b, e):
                if e == 0:
                    pe.wait_ge(s_rt, b * NRT + 6)
                if e >= 2 or not (isinstance(b, int) and b == 0):
                    pe.wait_ge(s_m, b * NE + (e - 1))
                split_product(ps_e[e % 2][:, :], lambda a, k: wa[:, a, k, RANK * e:RANK * e + RANK],
                              lambda c, k: yT[:, c, k, :], KC, True, True, s_e1)

            def second(b, e):
                pe.wait_ge(s_mlo, b * NE + (e + 1))
                for i in range(NT):
                    if e == 0:
                        if isinstance(b, int) and b == 0:
                            pe.wait_ge(s_x1, NB * NT)
                        else:
                            pe.wait_ge(s_out, (b - 1) * NT + (i + 1))
                    for n, (a, c) in enumerate(((0, 0), (0, 1), (1, 0))):
                        ins = t.matmul(ps_o[i][:, :], mT[:, e % 2, a, P * i:P * i + P], wb[:, c, e, :],
                                       start=e == 0 and n == 0, stop=e == NE - 1 and n == 2)
                ins.then_inc(s_e2, 1)

            def batch(b, following):
                router(b)
                pe.wait_ge(s_ylo, b + 1)
                first(b, 0)
                combine(b)
                spread(b, 0)
                for e in range(NE):
                    if e + 1 < NE:
                        first(b, e + 1)
                        spread(b, e + 1)
                    if following and e % 2 == 0:
                        j = (b + (NB + 1)) * KC + e // 2
                        cond_a(j, e // 2, lambda j: pe.wait_ge(s_sig, j))
                    second(b, e)

            pe.wait_ge(s_wlo, 2)
            for c in range(KC):
                cond_a(NB * KC + c, c, (lambda j: pe.wait_ge(s_ysrc, 4 * NB)) if c == 0 else
                       (lambda j: pe.wait_ge(s_sig, j)))
            batch(0, True)
            with pe.Fori(1, NB - 1) as b:
                batch(b, True)
            batch(NB - 1, False)


_INS = ['x', 'fside_BxSxS_0', 'cond_512', 'L0_cond_w', 'L0_cond_u', 'L0_ffn_gate_w', 'L0_ffn_up_w', 'L0_ffn_down_w',
        'L1_cond_w', 'L1_cond_u', 'L1_ffn_router_w', 'L1_ffn_Wa', 'L1_ffn_Wb']


def kernel(**inputs):
    import numpy as _np
    import concourse.bacc as _bacc
    from concourse import mybir as _mybir
    from concourse.bass_utils import run_bass_kernel_spmd as _run

    nc = _bacc.Bacc("TRN2", target_bir_lowering=False, num_devices=1)
    arrays, args = {}, []
    for name in _INS:
        a = _np.ascontiguousarray(inputs[name])
        arrays[f"in_{name}_dram"] = a
        args.append(nc.dram_tensor(f"in_{name}_dram", a.shape, _mybir.dt.from_np(a.dtype), kind="ExternalInput").ap())
    shape = inputs["x"].shape
    args.append(nc.dram_tensor("out_0_dram", shape, _mybir.dt.float32, kind="ExternalOutput").ap())
    adaln_ffn(nc, *args)
    r = _run(nc, [arrays], core_ids=[0])
    return r.results[0]["out_0_dram"]
```

```python
import math
from contextlib import ExitStack

import numpy as np

import concourse.bass as bass
from concourse import mybir

FP32 = mybir.dt.float32
FP16 = mybir.dt.float16
FP8R = mybir.dt.float8e5
ALU = mybir.AluOpType
ACT = mybir.ActivationFunctionType
AX = mybir.AxisListType


HALF, BACK = 2, 3
PIECES = {0: 0, 3: 1, 6: 2, 9: 3, 11: 4}
Y_AT = (7, 5, 3, 1)


def weight_units(q):
    return [("w", m, q, r) for m in range(3) for r in range(4)]


def first_steps():
    steps = [(u, n // 2 if n < 10 and n % 2 == 0 else None) for n, u in enumerate(weight_units(0))]
    return steps + [(("y", i), None) for i in range(4)]


def batch_steps(weights, following):
    steps, n = [], 0
    for q in range(4):
        more = weight_units(q + 1) if weights and q < 3 else []
        for i in range(4):
            steps.append((("h", q, i), PIECES.get(n)))
            steps += [(u, None) for u in more[3 * i:3 * i + 3]]
            if following and q == 3:
                steps.append((("y", i), None))
            n += 1
    return steps


def products(steps):
    plan = {k: [] for k in range(len(steps))}
    at = [k for k, (unit, _) in enumerate(steps) if unit[0] == "h"]
    nexts = at[1:] + ([len(steps)] if steps[-1][0][0] == "y" else [])
    for n, k in enumerate(nexts):
        if not at:
            gate, up = k - 1, k - 1
        elif n % 4 < 3:
            gate, up = at[n], min(at[n] + 1, k - 1)
        else:
            gate, up = max(at[n], k - 2), k - 1
        plan[gate].append(("gate", n + 1 if at else 16))
        plan[up].append(("up", n + 1 if at else 16))
    return plan


def adaln_ffn(nc, x, f, cond, w0, u0, gate_w, up_w, down_w, w1, u1, router_w, moe_a, moe_b, out):
    NB, T, C = x.shape
    P = 128
    KC = C // P
    NT = T // P
    I = gate_w.shape[0]
    NQ = I // 512
    NE, _, RANK = moe_a.shape
    BLK = 32
    NBLK = 512 // BLK
    assert (NT, KC, NQ, RANK) == (4, 4, 4, P)

    FP8_MAX = 448.0
    EPS = 1e-30
    E30 = float(np.exp(np.float32(30.0)))
    DOWN20 = 2.0 ** -20
    LEAST = 1.125 * 2.0 ** -6
    KY, KW, KH, KM = 8, 10, 10, 8

    PRO = first_steps()
    HEAD = batch_steps(True, True)
    MID = batch_steps(False, True)
    LAST = batch_steps(False, False)
    U_HEAD = len(PRO)
    U_MID = U_HEAD + len(HEAD)
    LM = len(MID)

    def units_before(b):
        return U_HEAD if isinstance(b, int) and b == 0 else (b - 1) * LM + U_MID

    x_t = x.rearrange("b (t p) c -> b p t c", p=P)
    f_t = f.rearrange("b (t p) c -> b p t c", p=P)
    out_t = out.rearrange("b (t p) c -> b p t c", p=P)
    x1_dram = nc.dram_tensor("x1_dram", [NB, P, NT, C], FP32, kind="Internal").ap()
    moe_a_v = moe_a.rearrange("e (k p) r -> p k e r", p=P)
    moe_b_v = moe_b.rearrange("e r c -> r e c")
    router_v = router_w.rearrange("(k p) e -> p k e", p=P)
    w_drams = (gate_w, up_w, down_w)

    ctx = ExitStack()
    with ctx:
        def sb(name, shape, dt=FP32):
            return ctx.enter_context(nc.sbuf_tensor(name, shape, dt))

        def sem(name):
            return ctx.enter_context(nc.semaphore(name))

        wg = sb("wg", [P, 2, NQ, KC, 512], FP16)
        wu = sb("wu", [P, 2, NQ, KC, 512], FP16)
        wd = sb("wd", [P, 2, NQ, 4, C], FP16)
        f_nat = sb("f_nat", [P, NT, C])
        x_nat = sb("x_nat", [P, NT, C])
        x_res = sb("x_res", [P, NT, C])
        fT = sb("fT", [P, T])
        th = sb("th", [P, 2, T])
        ek = sb("ek", [P, 2, T])
        eu = sb("eu", [P, T])
        ekv = sb("ekv", [P, T])
        fwd_n = sb("fwd_n", [P, T])
        fwd_d = sb("fwd_d", [P, T])
        rd = sb("rd", [P, T])
        num = sb("num", [P, T])
        y_ch = sb("y_ch", [P, KC, T])
        yT = sb("yT", [P, 2, KC, T], FP16)
        hT = sb("hT", [P, 2, 2, KC, P], FP16)
        src = sb("src", [P, 4, 512])
        qp = sb("qp", [P, 4, 512])
        rc = sb("rc", [P, 2, 512], FP8R)
        rr = sb("rr", [P, 4, 512])
        silu = sb("silu", [P, 2, 512])
        amax = sb("amax", [P, 2, NBLK])
        scale = sb("scale", [P, 4, NBLK])
        rinv = sb("rinv", [P, 4, NBLK])
        ident = sb("ident", [P, P])
        cond_sb = sb("cond_sb", [P, NB, P])
        csum = sb("csum", [P, NB])
        tf = sb("tf", [P, NB])
        half = sb("half", [P, NB])
        ncb = sb("ncb", [P, NB])
        wv = sb("wv", [P, 2, KC])
        uv = sb("uv", [P, 2, KC])
        ew = sb("ew", [P, 2, KC])
        dw = sb("dw", [P, 2, KC])
        dec = sb("dec", [P, 2, KC, NB])
        kb = sb("kb", [P, 2, KC, NB])
        gb = sb("gb", [P, 2, KC, NB])
        tmp1 = sb("tmp1", [P, 2, KC, NB])
        tmp2 = sb("tmp2", [P, 2, KC, NB])
        ini = sb("ini", [P, 2])
        nleast = sb("nleast", [P, 1])
        gap = sb("gap", [P, 5])
        def parts_of(w):
            return w[:, :, :, :, :].rearrange("p a q k n -> p a (q k n)")
        wa = parts_of(wg)[:, :, 0:KC * NE * RANK].rearrange("p a (k n) -> p a k n", k=KC)
        wb = parts_of(wu)[:, :, 0:NE * C].rearrange("p a (e n) -> p a e n", e=NE)

        def raw_at(w, part, at):
            return parts_of(w)[:, part, at:at + 2048].bitcast(FP32)
        wa_raw = [raw_at(w, part, 4096) for w in (wg, wu) for part in range(2)]
        wb_raw = [raw_at(wd, 0, 0), raw_at(wd, 0, 2048), raw_at(wd, 0, 4096), raw_at(wd, 1, 0)]
        sq = src
        cbs = silu
        ms = qp
        mT = hT[:, :, :, :, :].rearrange("p s a k t -> p s a (k t)")
        rw = sb("rw", [P, KC, NE])
        ones = sb("ones", [P, 2])
        onehot = sb("onehot", [NE, NE, P])
        lower = sb("lower", [P, NE, NE])
        ssq = sb("ssq", [P, NT])
        nrm = sb("nrm", [P, NT])
        nr1 = sb("nr1", [P, NT])
        nr2 = sb("nr2", [P, NT])
        lg = sb("lg", [P, NT, NE])
        mx = sb("mx", [P, NT])
        pe_ = sb("pe_", [P, NT, NE])
        zz = sb("zz", [P, NT])
        gt = sb("gt", [P, NT, NE, NE])
        eq = sb("eq", [P, NT, NE, NE])
        cnt = sb("cnt", [P, NT, NE])
        cmb = sb("cmb", [P, NT, NE])
        cmbT = sb("cmbT", [NE, T])

        def bank(name):
            return ctx.enter_context(nc.psum_tensor(name, [P, 512], FP32))
        ps_gate, ps_up, ps_t, ps_m = bank("ps_gate"), bank("ps_up"), bank("ps_t"), bank("ps_m")
        ps_o = [bank(f"ps_o{i}") for i in range(NT)]

        s_const = sem("s_const")
        s_par = sem("s_par")
        s_csum = sem("s_csum")
        s_tf = sem("s_tf")
        s_prep = sem("s_prep")
        s_dw = sem("s_dw")
        s_wload = [sem(f"s_wload{i}") for i in range(4)]
        s_fnat = sem("s_fnat")
        s_xnat = sem("s_xnat")
        s_xres = sem("s_xres")
        s_x1out = sem("s_x1out")
        s_ftr = sem("s_ftr")
        s_xtr = sem("s_xtr")
        s_fT = sem("s_fT")
        s_th = sem("s_th")
        s_ek = sem("s_ek")
        s_eu = sem("s_eu")
        s_cd = sem("s_cd")
        s_ln = sem("s_ln")
        s_rd = sem("s_rd")
        s_ytr = sem("s_ytr")
        s_ysrc = sem("s_ysrc")
        s_gate = sem("s_gate")
        s_up = sem("s_up")
        s_silu = sem("s_silu")
        s_h = sem("s_h")
        s_amax = sem("s_amax")
        s_scale = sem("s_scale")
        s_rinv = sem("s_rinv")
        s_qp = sem("s_qp")
        s_rc = sem("s_rc")
        s_rr = sem("s_rr")
        s_qt = sem("s_qt")
        s_pu = sem("s_pu")
        s_nq = sem("s_nq")
        s_deq = sem("s_deq")
        s_tr = sem("s_tr")
        s_hi = sem("s_hi")
        s_lo = sem("s_lo")
        s_down = sem("s_down")
        s_x1 = sem("s_x1")
        s_wa = [sem(f"s_wa{k}") for k in range(4)]
        s_wb = [sem(f"s_wb{k}") for k in range(4)]
        s_rwl = sem("s_rwl")
        s_whi = sem("s_whi")
        s_wlo = sem("s_wlo")
        s_yhi = sem("s_yhi")
        s_ylo = sem("s_ylo")
        s_sq = sem("s_sq")
        s_lgt = sem("s_lgt")
        s_rt = sem("s_rt")
        s_rc2 = sem("s_rc2")
        s_sqrt = sem("s_sqrt")
        s_exp = sem("s_exp")
        s_ctr = sem("s_ctr")
        s_cT = sem("s_cT")
        s_cb = sem("s_cb")
        s_cbs = sem("s_cbs")
        s_e1 = sem("s_e1")
        s_m = sem("s_m")
        s_mhi = sem("s_mhi")
        s_mlo = sem("s_mlo")
        s_e2 = sem("s_e2")
        s_out = sem("s_out")
        s_outd = sem("s_outd")

        NCD = 15
        NRT = 16

        def part_of(unit, k, part):
            if unit[0] == "w":
                _, m, q, r = unit
                return (wg, wu, wd)[m][:, part, q, :, P * r:P * r + P]
            if unit[0] == "y":
                return yT[:, part, :, P * unit[1]:P * unit[1] + P]
            n = 4 * unit[1] + unit[2]
            return hT[:, n % 2, part, :, :]

        tail = [("y", 2), ("h", 3, 3), ("y", 3)]
        power_of = {"w": KW, "y": KY, "h": KH}

        block = ctx.enter_context(nc.Block())

        @block.sync
        def _(sp):
            def load_weight(u, unit):
                _, m, q, r = unit
                if u >= 4:
                    sp.wait_ge(s_qp, u - 3)
                rows = w_drams[m][P * (4 * q + r):P * (4 * q + r + 1), :] if m < 2 else \
                    w_drams[m][P * r:P * (r + 1), 512 * q:512 * (q + 1)]
                sp.dma_start(src[:, u % 4, :], rows).then_inc(s_wload[u % 4], 16)

            def load_cond(j, b, source):
                if not (isinstance(j, int) and j == 0):
                    sp.wait_ge(s_ftr, j * KC)
                    sp.wait_ge(s_xtr, j * KC)
                sp.dma_start(f_nat[:, :, :], f_t[b]).then_inc(s_fnat, 16)
                sp.dma_start(x_nat[:, :, :], source[b]).then_inc(s_xnat, 16)

            def load_residual(j, b, source, done, value):
                if done is not None:
                    sp.wait_ge(done, value)
                sp.dma_start(x_res[:, :, :], source[b]).then_inc(s_xres, 16)

            sp.dma_start(cond_sb[:, :, :], cond.rearrange("(a b) d -> a b d", a=1).to_broadcast([P, NB, P]))\
                .then_inc(s_par, 16)
            for n, (w, u) in enumerate(((w0, u0), (w1, u1))):
                sp.dma_start(wv[:, n, :], w.rearrange("(k p) -> p k", p=P),
                             allow_slow_non_contiguous=True).then_inc(s_par, 16)
                sp.dma_start(uv[:, n, :], u.rearrange("(k p) -> p k", p=P),
                             allow_slow_non_contiguous=True).then_inc(s_par, 16)
            load_cond(0, 0, x_t)
            units = [unit for unit, _ in PRO + HEAD]
            for u in range(4):
                load_weight(u, units[u])
            load_residual(0, 0, x_t, None, 0)
            for u in range(4, U_MID):
                if u == U_HEAD:
                    load_cond(1, 1, x_t)
                if units[u][0] == "w":
                    load_weight(u, units[u])
            sp.dma_start(rw[:, :, :], router_v).then_inc(s_rwl, 16)

            def keep_x1(b):
                sp.wait_ge(s_x1, b * NT + NT)
                sp.dma_start(x1_dram[b], x_res[:, :, :]).then_inc(s_x1out, 16)

            with sp.Fori(1, NB - 1) as b:
                load_cond(b + 1, b + 1, x_t)
                keep_x1(b - 1)
                load_residual(b, b, x_t, s_x1out, b * 16)
            load_cond(NB, 0, x1_dram)
            keep_x1(NB - 2)
            load_residual(NB - 1, NB - 1, x_t, s_x1out, 16 * (NB - 1))
            sp.wait_ge(s_up, 16 * NB - 4)
            for k in range(KC):
                sp.dma_start(wa_raw[k].rearrange("p (e r) -> p e r", e=NE), moe_a_v[:, k, :, :]).then_inc(s_wa[k], 16)
            sp.wait_ge(s_down, 16 * NB - 4)
            for k in range(4):
                sp.dma_start(wb_raw[k].rearrange("p (e c) -> p e c", e=2), moe_b_v[:, 2 * k:2 * k + 2, :])\
                    .then_inc(s_wb[k], 16)
            keep_x1(NB - 1)
            load_residual(NB, 0, x1_dram, s_x1out, 16 * NB)

            def store_out(b):
                sp.wait_ge(s_out, b * NT + NT)
                sp.dma_start(out_t[b], x_res[:, :, :]).then_inc(s_outd, 16)

            with sp.Fori(0, NB - 1) as b:
                load_cond(b + (NB + 1), b + 1, x1_dram)
                store_out(b)
                load_residual(b, b + 1, x1_dram, s_outd, b * 16 + 16)
            store_out(NB - 1)
            sp.wait_ge(s_outd, 16 * NB)

        @block.gpsimd
        def _(pool):
            nc.gpsimd.memset(ident[:, :], 0.0).then_inc(s_const, 1)
            nc.gpsimd.memset(ones[:, :], 1.0).then_inc(s_const, 1)
            nc.gpsimd.memset(onehot[:, :, :], 0.0).then_inc(s_const, 1)
            nc.gpsimd.memset(lower[:, :, :], 1.0).then_inc(s_const, 1)
            pool.wait_ge(s_const, 4)
            nc.gpsimd.affine_select(out=ident[:, :], in_=ident[:, :], compare_op=ALU.not_equal, fill=1.0,
                                    base=0, pattern=[[-1, P]], channel_multiplier=1).then_inc(s_const, 1)
            nc.gpsimd.affine_select(out=onehot[:, :, :], in_=onehot[:, :, :], compare_op=ALU.not_equal, fill=1.0,
                                    base=0, pattern=[[-1, NE], [0, P]], channel_multiplier=1).then_inc(s_const, 1)
            nc.gpsimd.affine_select(out=lower[:, :, :], in_=lower[:, :, :], compare_op=ALU.is_gt, fill=0.0,
                                    base=0, pattern=[[1, NE], [-1, NE]], channel_multiplier=0).then_inc(s_const, 1)

            def blocks(ap):
                return ap.rearrange("p (n k) -> p n k", k=BLK)

            def spread(ap):
                return ap.unsqueeze(2).to_broadcast([P, NBLK, BLK])

            def normalise(u, k, unit):
                pool.wait_ge(s_rinv, u + 1)
                if not (isinstance(u, int) and u < 4):
                    pool.wait_ge(s_tr, u - 3)
                nc.gpsimd.tensor_tensor(blocks(qp[:, k % 4, :]), blocks(src[:, k % 4, :]),
                                        spread(rinv[:, k % 4, :]), ALU.mult).then_inc(s_qp, 1)

            def dequantise(u, k):
                pool.wait_ge(s_nq, u + 1)
                at = blocks(qp[:, k % 4, :])
                nc.gpsimd.tensor_tensor(at, at, spread(scale[:, k % 4, :]), ALU.mult).then_inc(s_deq, 1)

            def cond_a(j):
                pool.wait_ge(s_eu, j + 1)
                if not isinstance(j, int):
                    nc.gpsimd.tensor_tensor(gap[:, 4:5], nleast[:, 0:1], nleast[:, 0:1], ALU.add)
                nc.gpsimd.tensor_scalar(eu[:, :], eu[:, :], E30, None, ALU.min).then_inc(s_pu, 1)
                pool.wait_ge(s_pu, j * 2 + 1)
                pool.wait_ge(s_cd, j * NCD + 1)
                nc.gpsimd.tensor_tensor(fT[:, :], eu[:, :], fT[:, :], ALU.mult).then_inc(s_pu, 1)

            def run(steps, base, k0, j0):
                for k, (unit, piece) in enumerate(steps):
                    if k0 + k >= HALF:
                        dequantise(base + (k - HALF), k0 + k - HALF)
                    normalise(base + k, k0 + k, unit)
                    if k > 0 and steps[k - 1][1] in range(KC):
                        cond_a(j0 + steps[k - 1][1])

            run(PRO, 0, 0, 0)
            run(HEAD, U_HEAD, U_HEAD, KC)
            with pool.Fori(1, NB - 1) as b:
                run(MID, units_before(b), U_MID, b * KC + KC)
            uL = units_before(NB - 1)
            run(LAST, uL, U_MID, NB * KC)
            for n in range(16 - HALF, 16):
                dequantise(uL + n, U_MID + n)

            def low(b, e):
                pool.wait_ge(s_mhi, b * NE + (e + 1))
                nc.gpsimd.tensor_tensor(mT[:, e % 2, 1, :], ms[:, e % 2, :], mT[:, e % 2, 0, :], ALU.subtract)\
                    .then_inc(s_mlo, 1)

            def experts(b, following):
                for e in range(NE):
                    low(b, e)
                    if following and 1 <= e <= KC:
                        cond_a((b + (NB + 1)) * KC + (e - 1))

            experts(0, True)
            with pool.Fori(1, NB - 1) as b:
                experts(b, True)
            experts(NB - 1, False)

        @block.scalar
        def _(act):
            act.wait_ge(s_csum, 1)
            nc.scalar.activation(tf[:, :], csum[:, :], ACT.Sigmoid).then_inc(s_tf, 1)
            act.wait_ge(s_par, 5 * 16)
            nc.scalar.activation(ew[:, :, :], wv[:, :, :], ACT.Exp).then_inc(s_dw, 1)
            act.wait_ge(s_dw, 1)
            nc.scalar.activation(dw[:, :, :], ew[:, :, :], ACT.Exp, scale=-1.0).then_inc(s_dw, 1)

            def cond_x(j, c):
                act.wait_ge(s_ftr, j + 1)
                if not (isinstance(j, int) and j == 0):
                    act.wait_ge(s_cd, (j - 1) * NCD + 11)
                nc.scalar.activation(fT[:, :], ps_m[:, :], ACT.Copy).then_inc(s_fT, 1)

            def cond_tanh(j, c):
                act.wait_ge(s_xtr, j + 1)
                nc.scalar.activation(th[:, c % 2, :], ps_m[:, :], ACT.Tanh, scale=0.5).then_inc(s_th, 1)

            def cond_e(layer, j, c):
                act.wait_ge(s_fT, j + 1)
                nc.scalar.activation(ek[:, c % 2, :], fT[:, :], ACT.Exp).then_inc(s_ek, 1)
                nc.scalar.activation(eu[:, :], fT[:, :], ACT.Exp, bias=uv[:, layer, c:c + 1]).then_inc(s_eu, 1)

            def cond_ln(j, c):
                nc.scalar.preload_act_table_set("natural_log_exp_and_others")
                act.wait_ge(s_cd, j * NCD + 10)
                nc.scalar.activation(rd[:, :], ek[:, c % 2, :], ACT.Ln).then_inc(s_ln, 1)
                act.wait_ge(s_ln, j + 1)
                nc.scalar.activation(rd[:, :], rd[:, :], ACT.Exp, scale=-1.0).then_inc(s_rd, 1)

            def piece_of(layer, j0, c):
                if c < KC:
                    cond_x(j0 + c, c)
                if c > 0:
                    cond_ln(j0 + (c - 1), c - 1)
                if c < KC:
                    cond_e(layer, j0 + c, c)

            def high(u, k, unit, g0):
                act.wait_ge(s_tr, u + 1)
                if unit[0] == "h":
                    n = 4 * unit[1] + unit[2]
                    if not (isinstance(g0, int) and g0 + n < 2):
                        act.wait_ge(s_down, g0 + n - 1)
                nc.scalar.activation(part_of(unit, k, 0), ps_t[:, :].rearrange("p (k t) -> p k t", k=4), ACT.Copy,
                                     scale=-(2.0 ** power_of[unit[0]]))\
                    .then_inc(s_hi, 1)

            def carry(u, column):
                if not isinstance(u, int):
                    nc.scalar.activation(gap[:, column:column + 1], nleast[:, 0:1], ACT.Copy)

            def round_constant(u, k):
                act.wait_ge(s_qp, u + 1)
                carry(u, 2 * (k % 2))
                nc.scalar.activation(rc[:, k % 2, :], qp[:, k % 4, :], ACT.Abs, scale=0.9375 / DOWN20,
                                     saturate=False).then_inc(s_rc, 1)
                act.wait_ge(s_rc, u + 1)
                carry(u, 2 * (k % 2) + 1)
                nc.scalar.activation(rr[:, k % 4, :], rc[:, k % 2, :], ACT.Relu, scale=1.125, bias=nleast[:, 0:1])\
                    .then_inc(s_rr, 1)

            def own(u, k, unit, g0, y0):
                if unit[0] == "h":
                    n = 4 * unit[1] + unit[2]
                    act.wait_ge(s_gate, g0 + n + 1)
                    if not (isinstance(g0, int) and g0 + n < 2):
                        act.wait_ge(s_h, g0 + n - 1)
                    nc.scalar.activation(silu[:, n % 2, :], ps_gate[:, :], ACT.Silu, scale=2.0 ** -(KY + KW))\
                        .then_inc(s_silu, 1)
                if unit[0] == "y":
                    act.wait_ge(s_ytr, y0 + unit[1] + 1)
                    act.wait_ge(s_qp, u - 3)
                    nc.scalar.activation(src[:, k % 4, :], ps_m[:, :], ACT.Copy).then_inc(s_ysrc, 1)

            def run(steps, base, k0, before, g0, y0, j0, layer=0):
                units = before + [unit for unit, _ in steps]
                nb = len(before)
                for k, (unit, piece) in enumerate(steps):
                    own(base + k, k0 + k, unit, g0, y0)
                    if k0 + k >= BACK:
                        high(base + (k - BACK), k0 + k - BACK, units[nb + k - BACK], g0 if k >= BACK else g0 - 16)
                    if k0 + k >= 1:
                        round_constant(base + (k - 1), k0 + k - 1)
                    if k > 0 and steps[k - 1][1] in range(KC):
                        cond_tanh(j0 + steps[k - 1][1], steps[k - 1][1])
                    if piece is not None:
                        piece_of(layer, j0, piece)

            run(PRO, 0, 0, [], 0, 0, 0)
            run(HEAD, U_HEAD, U_HEAD, [("y", 1), ("y", 2), ("y", 3)], 0, 4, 4)
            with act.Fori(1, NB - 1) as b:
                run(MID, units_before(b), U_MID, tail, b * 16, b * 4 + 4, b * 4 + 4)
            uL, gL = units_before(NB - 1), 16 * (NB - 1)

            def split_high(dst, raw, landed, part_free=None):
                act.wait_ge(landed, 16)
                nc.scalar.activation(dst, raw, ACT.Copy, scale=2.0 ** KM).then_inc(s_whi, 1)

            run(LAST, uL, U_MID, tail, gL, 4 * NB, 4 * NB, 1)
            high(uL + 13, U_MID + 13, ("h", 3, 1), gL)
            round_constant(uL + 15, U_MID + 15)

            def squares(b):
                act.wait_ge(s_cd, (b + NB + 1) * KC * NCD)
                nc.scalar.activation(sq[:, :, :], y_ch[:, :, :], ACT.Square).then_inc(s_sq, 1)

            def y_high(b):
                nc.scalar.activation(yT[:, 0, :, :], y_ch[:, :, :], ACT.Copy, scale=2.0 ** KM).then_inc(s_yhi, 1)

            def router(b):
                act.wait_ge(s_rt, b * NRT + 1)
                nc.scalar.activation(nrm[:, :], ssq[:, :], ACT.Sqrt).then_inc(s_sqrt, 1)
                act.wait_ge(s_rt, b * NRT + 8)
                nc.scalar.activation(pe_[:, :, :], lg[:, :, :], ACT.Exp).then_inc(s_exp, 1)
                act.wait_ge(s_ctr, b + 1)
                nc.scalar.activation(cmbT[:, :], ps_t[0:NE, :], ACT.Copy).then_inc(s_cT, 1)

            def spread_copy(b, e):
                act.wait_ge(s_cb, b * NE + (e + 1))
                if e >= 2 or not (isinstance(b, int) and b == 0):
                    act.wait_ge(s_m, b * NE + (e - 1))
                nc.scalar.activation(cbs[:, e % 2, :], ps_t[:, :], ACT.Copy).then_inc(s_cbs, 1)

            def expert_high(b, e):
                act.wait_ge(s_m, b * NE + (e + 1))
                if e >= 2 or not (isinstance(b, int) and b == 0):
                    act.wait_ge(s_e2, b * NE + (e - 1))
                nc.scalar.activation(mT[:, e % 2, 0, :], ms[:, e % 2, :], ACT.Copy).then_inc(s_mhi, 1)

            def experts(b, following):
                spread_copy(b, 0)
                for e in range(NE):
                    if e + 1 < NE:
                        spread_copy(b, e + 1)
                    if following and e == NE - 1:
                        squares(b + 1)
                    expert_high(b, e)
                    if following and 1 <= e <= KC:
                        cond_tanh((b + (NB + 1)) * KC + (e - 1), e - 1)
                    if following and e <= KC:
                        piece_of(1, (b + (NB + 1)) * KC, e)
                if following:
                    act.wait_ge(s_e1, b * NE + NE)
                    y_high(b + 1)
                    router(b + 1)

            for k in range(KC):
                split_high(wa[:, 0, k, :], wa_raw[k], s_wa[k])
            high(uL + 14, U_MID + 14, ("h", 3, 2), gL)
            act.wait_ge(s_qp, uL + 16)
            squares(0)
            act.wait_ge(s_up, 16 * NB)
            y_high(0)
            high(uL + 15, U_MID + 15, ("h", 3, 3), gL)
            for k in range(4):
                split_high(wb[:, 0, 2 * k:2 * k + 2, :].rearrange("p e n -> p (e n)"), wb_raw[k], s_wb[k])
            router(0)
            experts(0, True)
            with act.Fori(1, NB - 1) as b:
                experts(b, True)
            experts(NB - 1, False)

        @block.vector
        def _(dve):
            v = nc.vector
            n = [0]

            def link(ins):
                n[0] += 1
                ins.then_inc(s_prep, 1)
                dve.wait_ge(s_prep, n[0])

            v.memset(nleast[:, :], -LEAST).then_inc(s_prep, 1)
            n[0] += 1
            dve.wait_ge(s_par, 5 * 16)
            v.tensor_reduce(csum[:, :], cond_sb[:, :, :], AX.X, ALU.add).then_inc(s_csum, 1)
            dve.wait_ge(s_tf, 1)
            link(v.tensor_scalar(half[:, :], tf[:, :], 0.5, 0.5, ALU.mult, ALU.add))
            link(v.tensor_scalar(ncb[:, :], tf[:, :], -0.1, -0.4, ALU.mult, ALU.add))
            dve.wait_ge(s_dw, 2)
            for layer in range(2):
                link(v.tensor_tensor(dec[:, layer], dw[:, layer].unsqueeze(2).to_broadcast([P, KC, NB]),
                                     half[:, :].unsqueeze(1).to_broadcast([P, KC, NB]), ALU.mult))
            link(v.tensor_scalar(tmp1[:, :, :, :], dec[:, :, :, :], -1.0, 1.0, ALU.mult, ALU.add))
            link(v.tensor_scalar(tmp2[:, :, :, :], dec[:, :, :, :], 1.0, None, ALU.add))
            link(v.tensor_tensor(tmp1[:, :, :, :], tmp1[:, :, :, :], tmp2[:, :, :, :], ALU.mult))
            link(v.tensor_scalar(kb[:, :, :, :], tmp1[:, :, :, :], 1e-12, None, ALU.max))
            link(v.reciprocal(tmp2[:, :, :, :], kb[:, :, :, :]))
            link(v.tensor_tensor(gb[:, :, :, :], dec[:, :, :, :], tmp2[:, :, :, :], ALU.mult))

            def cond_a(layer, j, c, b):
                at = j * NCD
                e = ek[:, c % 2, :]
                e_back = ek[:, c % 2, ::-1]
                dd = dec[:, layer, c, bass.ds(b, 1)].to_broadcast([P, T])
                g = gb[:, layer, c, bass.ds(b, 1)]
                k = kb[:, layer, c, bass.ds(b, 1)]

                def did(ins):
                    ins.then_inc(s_cd, 1)
                dve.wait_ge(s_ek, j + 1)
                did(v.scalar_tensor_tensor(out=ekv[:, :], in0=e, scalar=E30, in1=fT[:, :],
                                           op0=ALU.min, op1=ALU.mult))
                did(v.tensor_scalar(e, e, E30, None, ALU.min))
                dve.wait_ge(s_cd, at + 1)
                did(v.tensor_tensor_scan(fwd_n[:, :], dd, ekv[:, :], 0.0, ALU.mult, ALU.add))
                dve.wait_ge(s_cd, at + 2)
                did(v.tensor_tensor_scan(fwd_d[:, :], dd, e, 0.0, ALU.mult, ALU.add))
                dve.wait_ge(s_cd, at + 3)
                did(v.tensor_tensor(ini[:, 0:1], fwd_n[:, T - 1:T], g, ALU.mult))
                dve.wait_ge(s_cd, at + 4)
                did(v.tensor_tensor(ini[:, 1:2], fwd_d[:, T - 1:T], g, ALU.mult))
                dve.wait_ge(s_cd, at + 6)
                did(v.tensor_tensor_scan(e_back, dd, fwd_d[:, ::-1], ini[:, 1:2], ALU.mult, ALU.add))
                did(v.tensor_tensor_scan(ekv[:, ::-1], dd, fwd_n[:, ::-1], ini[:, 0:1], ALU.mult, ALU.add))
                dve.wait_ge(s_pu, j * 2 + 2)
                dve.wait_ge(s_cd, at + 7)
                did(v.scalar_tensor_tensor(out=fwd_d[:, :], in0=e, scalar=k, in1=eu[:, :],
                                           op0=ALU.mult, op1=ALU.add))
                dve.wait_ge(s_cd, at + 9)
                did(v.tensor_scalar(e, fwd_d[:, :], 1e-8, None, ALU.max))
                did(v.scalar_tensor_tensor(out=num[:, :], in0=ekv[:, :], scalar=k, in1=fT[:, :],
                                           op0=ALU.mult, op1=ALU.add))

            def cond_b(layer, j, c, b, y_free):
                at = j * NCD
                e = ek[:, c % 2, :]

                def did(ins):
                    ins.then_inc(s_cd, 1)
                dve.wait_ge(s_th, j + 1)
                dve.wait_ge(s_cd, at + 11)
                did(v.scalar_tensor_tensor(out=num[:, :], in0=th[:, c % 2, :], scalar=1.0, in1=num[:, :],
                                           op0=ALU.add, op1=ALU.mult))
                dve.wait_ge(s_rd, j + 1)
                v.tensor_tensor(fwd_d[:, :], e, rd[:, :], ALU.mult).then_inc(s_cd, 1)
                dve.wait_ge(s_cd, at + 13)
                v.scalar_tensor_tensor(out=fwd_d[:, :], in0=fwd_d[:, :], scalar=2.0, in1=rd[:, :],
                                       op0=ALU.subtract, op1=ALU.mult).then_inc(s_cd, 1)
                dve.wait_ge(s_cd, at + 14)
                if c == 0:
                    y_free()
                v.scalar_tensor_tensor(out=y_ch[:, c, :], in0=num[:, :], scalar=ncb[:, bass.ds(b, 1)],
                                       in1=fwd_d[:, :], op0=ALU.mult, op1=ALU.mult).then_inc(s_cd, 1)

            def piece_of(layer, j0, c, b, y_free):
                if c > 0:
                    cond_b(layer, j0 + (c - 1), c - 1, b, y_free)
                if c < KC:
                    cond_a(layer, j0 + c, c, b)

            def blocks(ap):
                return ap.rearrange("p (n k) -> p n k", k=BLK)

            def low(u, k, unit):
                dve.wait_ge(s_hi, u + 1)
                v.scalar_tensor_tensor(out=part_of(unit, k, 1), in0=ps_t[:, :].rearrange("p (k t) -> p k t", k=4),
                                       scalar=-(2.0 ** power_of[unit[0]]), in1=part_of(unit, k, 0),
                                       op0=ALU.mult, op1=ALU.subtract).then_inc(s_lo, 1)

            def round_up(u, k):
                dve.wait_ge(s_rr, u + 1)
                q = qp[:, k % 4, :]
                v.scalar_tensor_tensor(out=q, in0=rr[:, k % 4, :], scalar=LEAST, in1=q,
                                       op0=ALU.add, op1=ALU.add).then_inc(s_qt, 1)

            def round_off(u, k):
                dve.wait_ge(s_qt, u + 1)
                q = qp[:, k % 4, :]
                v.scalar_tensor_tensor(out=q, in0=rr[:, k % 4, :], scalar=LEAST, in1=q,
                                       op0=ALU.add, op1=ALU.subtract).then_inc(s_nq, 1)

            def largest(u, k, unit, g0, y0, loads):
                if unit[0] == "h":
                    m = 4 * unit[1] + unit[2]
                    dve.wait_ge(s_silu, g0 + m + 1)
                    dve.wait_ge(s_up, g0 + m + 1)
                    v.scalar_tensor_tensor(out=src[:, k % 4, :], in0=ps_up[:, :], scalar=2.0 ** -(KY + KW),
                                           in1=silu[:, m % 2, :], op0=ALU.mult, op1=ALU.mult).then_inc(s_h, 1)
                    dve.wait_ge(s_h, g0 + m + 1)
                elif unit[0] == "y":
                    dve.wait_ge(s_ysrc, y0 + unit[1] + 1)
                else:
                    loads[k % 4] += 16
                    dve.wait_ge(s_wload[k % 4], loads[k % 4])
                v.tensor_reduce(amax[:, k % 2, :], blocks(src[:, k % 4, :]), AX.X, ALU.max,
                                apply_absolute_value=True).then_inc(s_amax, 1)

            def scales(u, k):
                dve.wait_ge(s_amax, u + 1)
                if not (isinstance(u, int) and u < 4):
                    dve.wait_ge(s_deq, u - 3)
                v.tensor_scalar(scale[:, k % 4, :], amax[:, k % 2, :], 1.0 / (FP8_MAX * DOWN20), EPS / DOWN20,
                                ALU.mult, ALU.max).then_inc(s_scale, 1)

            def inverses(u, k):
                dve.wait_ge(s_scale, u + 1)
                v.reciprocal(rinv[:, k % 4, :], scale[:, k % 4, :]).then_inc(s_rinv, 1)

            def sum_x1(b, i):
                dve.wait_ge(s_down, b * 16 + (13 + i))
                if i == 0:
                    dve.wait_ge(s_xres, b * 16 + 16)
                v.scalar_tensor_tensor(out=x_res[:, i, :], in0=ps_o[i][:, :], scalar=2.0 ** -(KH + KW),
                                       in1=x_res[:, i, :], op0=ALU.mult, op1=ALU.add).then_inc(s_x1, 1)

            def run(steps, base, k0, before, g0, y0, j0, b, loads, layer=0, y_free=None, sums=None):
                units = before + [unit for unit, _ in steps]
                nb = len(before)
                for k, (unit, piece) in enumerate(steps):
                    n, at = k0 + k, base + k
                    if n >= HALF:
                        round_up(at - HALF, n - HALF)
                    products_run = steps[0][0][0] == "h" and unit[0] != "w"
                    if products_run:
                        low(at - BACK, n - BACK, units[nb + k - BACK])
                    else:
                        largest(at, n, unit, g0, y0, loads)
                    if n >= HALF:
                        round_off(at - HALF, n - HALF)
                    if products_run:
                        largest(at, n, unit, g0, y0, loads)
                    scales(at, n)
                    if not products_run and n >= BACK:
                        low(at - BACK, n - BACK, units[nb + k - BACK])
                    inverses(at, n)
                    if sums is not None and k == 2:
                        for i in range(NT):
                            sum_x1(sums, i)
                    if k > 0 and steps[k - 1][1] is not None:
                        piece_of(layer, j0, steps[k - 1][1], b, y_free)

            loads = [0] * 4
            run(PRO, 0, 0, [], 0, 0, 0, 0, loads, y_free=lambda: None)
            run(HEAD, U_HEAD, U_HEAD, [("y", 1), ("y", 2), ("y", 3)], 0, 4, 4, 1, loads, y_free=lambda: dve.wait_ge(s_ytr, 4))
            with dve.Fori(1, NB - 1) as b:
                run(MID, units_before(b), U_MID, tail, b * 16, b * 4 + 4, b * 4 + 4, b + 1, loads,
                    y_free=lambda: dve.wait_ge(s_ytr, b * 4 + 4), sums=b - 1)
            uL, gL = units_before(NB - 1), 16 * (NB - 1)
            run(LAST, uL, U_MID, tail, gL, 4 * NB, 4 * NB, 0, loads, layer=1,
                y_free=lambda: dve.wait_ge(s_ytr, 4 * NB), sums=NB - 2)

            def split_low(dst, raw, high_, n):
                dve.wait_ge(s_whi, n)
                v.scalar_tensor_tensor(out=dst, in0=raw, scalar=2.0 ** KM, in1=high_,
                                       op0=ALU.mult, op1=ALU.subtract).then_inc(s_wlo, 1)

            def y_low(b):
                dve.wait_ge(s_yhi, b + 1)
                v.scalar_tensor_tensor(out=yT[:, 1, :, :].rearrange("p k t -> p (k t)"),
                                       in0=y_ch[:, :, :].rearrange("p k t -> p (k t)"), scalar=2.0 ** KM,
                                       in1=yT[:, 0, :, :].rearrange("p k t -> p (k t)"),
                                       op0=ALU.mult, op1=ALU.subtract).then_inc(s_ylo, 1)

            def router(b):
                at = b * NRT
                m = [0]

                def did(ins):
                    m[0] += 1
                    ins.then_inc(s_rt, 1)
                    dve.wait_ge(s_rt, at + m[0])
                over_e = [P, NT, NE]
                dve.wait_ge(s_lgt, b + 1)
                lgs = ps_t[:, 0:NT * 16].rearrange("p (i n) -> p i n", n=16)
                did(v.tensor_scalar(ssq[:, :], lgs[:, :, NE], 1e-24, None, ALU.max))
                dve.wait_ge(s_sqrt, b + 1)
                did(v.reciprocal(nr1[:, :], nrm[:, :]))
                did(v.tensor_tensor(nr1[:, :], nr1[:, :], ssq[:, :], ALU.mult))
                did(v.tensor_tensor(nr1[:, :], nr1[:, :], nrm[:, :], ALU.add))
                did(v.reciprocal(nr2[:, :], nr1[:, :]))
                did(v.scalar_tensor_tensor(out=lg[:, :, :], in0=lgs[:, :, 0:NE], scalar=2.0,
                                           in1=nr2[:, :].unsqueeze(2).to_broadcast(over_e),
                                           op0=ALU.mult, op1=ALU.mult))
                did(v.tensor_reduce(mx[:, :], lg[:, :, :], AX.X, ALU.max))
                did(v.tensor_tensor(lg[:, :, :], lg[:, :, :], mx[:, :].unsqueeze(2).to_broadcast(over_e),
                                    ALU.subtract))
                dve.wait_ge(s_exp, b + 1)
                did(v.tensor_reduce(zz[:, :], pe_[:, :, :], AX.X, ALU.add))
                did(v.reciprocal(mx[:, :], zz[:, :]))
                did(v.tensor_tensor(pe_[:, :, :], pe_[:, :, :], mx[:, :].unsqueeze(2).to_broadcast(over_e),
                                    ALU.mult))
                mine = pe_[:, :, :].unsqueeze(3).to_broadcast([P, NT, NE, NE])
                theirs = pe_[:, :, :].unsqueeze(2).to_broadcast([P, NT, NE, NE])
                v.tensor_tensor(gt[:, :, :, :], theirs, mine, ALU.is_gt).then_inc(s_rc2, 1)
                v.tensor_tensor(eq[:, :, :, :], theirs, mine, ALU.is_equal).then_inc(s_rc2, 1)
                dve.wait_ge(s_rc2, b * 4 + 2)
                v.tensor_tensor(eq[:, :, :, :], eq[:, :, :, :],
                                lower[:, :, :].unsqueeze(1).to_broadcast([P, NT, NE, NE]), ALU.mult)\
                    .then_inc(s_rc2, 1)
                dve.wait_ge(s_rc2, b * 4 + 3)
                v.tensor_tensor(gt[:, :, :, :], gt[:, :, :, :], eq[:, :, :, :], ALU.add).then_inc(s_rc2, 1)
                dve.wait_ge(s_rc2, b * 4 + 4)
                did(v.tensor_reduce(cnt[:, :, :], gt[:, :, :, :], AX.X, ALU.add))
                did(v.scalar_tensor_tensor(out=cmb[:, :, :], in0=cnt[:, :, :], scalar=1.5, in1=pe_[:, :, :],
                                           op0=ALU.is_lt, op1=ALU.mult))
                did(v.tensor_reduce(zz[:, :], cmb[:, :, :], AX.X, ALU.add))
                did(v.reciprocal(mx[:, :], zz[:, :]))
                did(v.tensor_tensor(cmb[:, :, :], cmb[:, :, :], mx[:, :].unsqueeze(2).to_broadcast(over_e),
                                    ALU.mult))
                assert m[0] == NRT

            ps_e = (ps_gate, ps_up)

            def expert(b, e):
                dve.wait_ge(s_e1, b * NE + (e + 1))
                dve.wait_ge(s_cbs, b * NE + (e + 1))
                if e >= 2 or not (isinstance(b, int) and b == 0):
                    dve.wait_ge(s_mlo, b * NE + (e - 1))
                v.scalar_tensor_tensor(out=ms[:, e % 2, :], in0=ps_e[e % 2][:, :], scalar=2.0 ** -KM,
                                       in1=cbs[:, e % 2, :], op0=ALU.mult, op1=ALU.mult).then_inc(s_m, 1)

            def finish(b):
                dve.wait_ge(s_xres, (b + NB) * 16 + 16)
                dve.wait_ge(s_e2, b * NE + NE)
                for i in range(NT):
                    v.scalar_tensor_tensor(out=x_res[:, i, :], in0=ps_o[i][:, :], scalar=2.0 ** -(2 * KM),
                                           in1=x_res[:, i, :], op0=ALU.mult, op1=ALU.add).then_inc(s_out, 1)

            def y_used(b):
                def wait():
                    dve.wait_ge(s_lgt, b + 1)
                    dve.wait_ge(s_ylo, b + 1)
                    dve.wait_ge(s_sq, b + 1)
                return wait

            def experts(b, following):
                for e in range(NE):
                    expert(b, e)
                    if following and 1 <= e <= KC + 1:
                        piece_of(1, (b + (NB + 1)) * KC, e - 1, b + 1, y_used(b))
                if following:
                    y_low(b + 1)
                    router(b + 1)
                finish(b)

            low(uL + 13, U_MID + 13, ("h", 3, 1))
            for n in (14, 15):
                round_up(uL + n, U_MID + n)
                round_off(uL + n, U_MID + n)
            for k in range(KC):
                split_low(wa[:, 1, k, :], wa_raw[k], wa[:, 0, k, :], k + 1)
            low(uL + 14, U_MID + 14, ("h", 3, 2))
            y_low(0)
            low(uL + 15, U_MID + 15, ("h", 3, 3))
            for k in range(4):
                e2 = slice(2 * k, 2 * k + 2)
                split_low(wb[:, 1, e2, :].rearrange("p e n -> p (e n)"), wb_raw[k],
                          wb[:, 0, e2, :].rearrange("p e n -> p (e n)"), KC + k + 1)
            router(0)
            for i in range(NT):
                sum_x1(NB - 1, i)
            experts(0, True)
            with dve.Fori(1, NB - 1) as b:
                experts(b, True)
            experts(NB - 1, False)

        @block.tensor
        def _(pe):
            t = nc.tensor
            pe.wait_ge(s_const, 7)

            def split_product(bank_, lhs, rhs, nk, first, last, done=None):
                for k in range(nk):
                    for n, (a, c) in enumerate(((0, 0), (0, 1), (1, 0))):
                        ins = t.matmul(bank_, lhs(a, k), rhs(c, k), start=first and k == 0 and n == 0,
                                       stop=last and k == nk - 1 and n == 2)
                if done is not None:
                    ins.then_inc(done, 1)

            def transpose4(bank_, tiles, done):
                for i, tile in enumerate(tiles):
                    ins = t.transpose(bank_[:, P * i:P * i + P], tile, ident[:, :])
                ins.then_inc(done, 1)

            def cond_f(j, c, bank_free):
                if c == 0:
                    pe.wait_ge(s_fnat, (j // KC) * 16 + 16 if isinstance(j, int) else j * 4 + 16)
                bank_free(j)
                transpose4(ps_m, [f_nat[:, i, P * c:P * c + P] for i in range(NT)], s_ftr)

            def cond_x(j, c):
                if c == 0:
                    pe.wait_ge(s_xnat, ((j // KC) * 16 + 16) if isinstance(j, int) else j * 4 + 16)
                pe.wait_ge(s_fT, j + 1)
                transpose4(ps_m, [x_nat[:, i, P * c:P * c + P] for i in range(NT)], s_xtr)

            def product(what, g, n):
                q, i = n // 4 % 4, n % 4
                w, bank_, read, done = (wg, ps_gate, s_silu, s_gate) if what == "gate" else (wu, ps_up, s_h, s_up)
                if not (isinstance(g, int) and g == 0):
                    pe.wait_ge(read, g)
                split_product(bank_[:, :], lambda a, k: yT[:, a, k, P * i:P * i + P],
                              lambda c, k: w[:, c, q, k, :], KC, True, True, done)

            def down(u, q, i, b):
                pe.wait_ge(s_lo, u + 1)
                if q == 0 and not (isinstance(b, int) and b == 0):
                    pe.wait_ge(s_x1, (b - 1) * NT + (i + 1))
                n = (4 * q + i) % 2
                split_product(ps_o[i][:, :], lambda a, k: hT[:, n, a, k, :], lambda c, k: wd[:, c, q, k, :],
                              4, q == 0, q == NQ - 1, s_down)

            def parts(u, k):
                pe.wait_ge(s_deq, u + 1)
                if not (isinstance(u, int) and u == 0):
                    pe.wait_ge(s_lo, u)
                transpose4(ps_t, [qp[:, k % 4, P * n:P * n + P] for n in range(4)], s_tr)

            def run(steps, base, k0, before, g0, y0, j0, b, ready):
                units = before + [unit for unit, _ in steps]
                nb = len(before)
                plan = products(steps)
                for k, (unit, piece) in enumerate(steps):
                    if unit[0] == "y":
                        i = unit[1]
                        if i == 0:
                            pe.wait_ge(s_cd, (j0 + KC) * NCD)
                            pe.wait_ge(s_th, j0 + KC)
                        else:
                            pe.wait_ge(s_ysrc, y0 + i)
                        transpose4(ps_m, [y_ch[:, c, P * i:P * i + P] for c in range(KC)], s_ytr)
                    if piece is not None and piece < KC:
                        def free(j, c=piece):
                            if c > 0:
                                pe.wait_ge(s_th, j)
                            elif not (isinstance(y0, int) and y0 == 0):
                                pe.wait_ge(s_ysrc, y0)
                        cond_f(j0 + piece, piece, free)
                    if k > 0 and steps[k - 1][1] in range(KC):
                        cond_x(j0 + steps[k - 1][1], steps[k - 1][1])
                    if k0 + k >= HALF:
                        parts(base + (k - HALF), k0 + k - HALF)
                    for what, n in plan[k]:
                        if what == "gate":
                            if n in ready:
                                pe.wait_ge(s_lo, base + ready[n])
                            product(what, g0 + n, n)
                    if k0 + k >= BACK:
                        past = units[nb + k - BACK]
                        if past[0] == "h":
                            down(base + (k - BACK), past[1], past[2], b if k >= BACK else b - 1)
                    for what, n in plan[k]:
                        if what == "up":
                            product(what, g0 + n, n)

            places = {unit: n for n, (unit, _) in enumerate(HEAD)}
            ready_pro = {16: U_HEAD - 3}
            ready_head = {i: i - 3 for i in range(1, 4)}
            for q in range(1, NQ):
                ready_head[4 * q] = max(places["w", m, q, r] for m in range(2) for r in range(4)) + 1
            ready_head[16] = len(HEAD) - Y_AT[0] + 1
            ready_mid = {i: 1 - Y_AT[i] for i in range(1, 4)}
            ready_mid[16] = LM - Y_AT[0] + 1

            run(PRO, 0, 0, [], -16, 0, 0, 0, ready_pro)
            run(HEAD, U_HEAD, U_HEAD, [("y", 1), ("y", 2), ("y", 3)], 0, 4, 4, 0, ready_head)
            with pe.Fori(1, NB - 1) as b:
                run(MID, units_before(b), U_MID, tail, b * 16, b * 4 + 4, b * 4 + 4, b, ready_mid)
            uL, gL = units_before(NB - 1), 16 * (NB - 1)
            run(LAST, uL, U_MID, tail, gL, 4 * NB, 4 * NB, NB - 1, ready_mid)
            parts(uL + 14, U_MID + 14)
            down(uL + 13, 3, 1, NB - 1)
            parts(uL + 15, U_MID + 15)

            ps_e = (ps_gate, ps_up)

            def router(b):
                pe.wait_ge(s_rwl, 16)
                pe.wait_ge(s_sq, b + 1)
                if isinstance(b, int) and b == 0:
                    pe.wait_ge(s_lo, uL + 16)
                else:
                    pe.wait_ge(s_cbs, b * NE)
                for i in range(NT):
                    for k in range(KC):
                        t.matmul(ps_t[:, 16 * i:16 * i + NE], y_ch[:, k, P * i:P * i + P], rw[:, k, :],
                                 start=k == 0, stop=k == KC - 1)
                    for k in range(KC):
                        ins = t.matmul(ps_t[:, 16 * i + NE:16 * i + NE + 2], sq[:, k, P * i:P * i + P], ones[:, :],
                                       start=k == 0, stop=k == KC - 1)
                ins.then_inc(s_lgt, 1)

            def combine(b):
                pe.wait_ge(s_rt, b * NRT + NRT)
                for i in range(NT):
                    ins = t.transpose(ps_t[0:NE, P * i:P * i + P], cmb[:, i, :], ident[:, :])
                ins.then_inc(s_ctr, 1)

            def spread(b, e):
                if e == 0:
                    pe.wait_ge(s_cT, b + 1)
                else:
                    pe.wait_ge(s_cbs, b * NE + e)
                t.matmul(ps_t[:, :], onehot[:, e, :], cmbT[:, :], start=True, stop=True).then_inc(s_cb, 1)

            def first(b, e):
                if e < 2 and isinstance(b, int) and b == 0:
                    pe.wait_ge(s_silu if e == 0 else s_h, 16 * NB)
                else:
                    pe.wait_ge(s_m, b * NE + (e - 1))
                split_product(ps_e[e % 2][:, :], lambda a, k: wa[:, a, k, RANK * e:RANK * e + RANK],
                              lambda c, k: yT[:, c, k, :], KC, True, True, s_e1)

            def second(b, e):
                pe.wait_ge(s_mlo, b * NE + (e + 1))
                for i in range(NT):
                    if e == 0:
                        if isinstance(b, int) and b == 0:
                            pe.wait_ge(s_x1, NB * NT)
                        else:
                            pe.wait_ge(s_out, (b - 1) * NT + (i + 1))
                    for n, (a, c) in enumerate(((0, 0), (0, 1), (1, 0))):
                        ins = t.matmul(ps_o[i][:, :], mT[:, e % 2, a, P * i:P * i + P], wb[:, c, e, :],
                                       start=e == 0 and n == 0, stop=e == NE - 1 and n == 2)
                ins.then_inc(s_e2, 1)

            def batch(b, following):
                pe.wait_ge(s_ylo, b + 1)
                first(b, 0)
                combine(b)
                spread(b, 0)
                for e in range(NE):
                    if e + 1 < NE:
                        first(b, e + 1)
                        spread(b, e + 1)
                    if following and 1 <= e <= KC:
                        cond_x((b + (NB + 1)) * KC + (e - 1), e - 1)
                    if following and e < KC:
                        cond_f((b + (NB + 1)) * KC + e, e, lambda j: pe.wait_ge(s_th, j))
                    if following and e == NE - 1:
                        router(b + 1)
                    second(b, e)

            router(0)
            down(uL + 14, 3, 2, NB - 1)
            down(uL + 15, 3, 3, NB - 1)
            pe.wait_ge(s_wlo, 8)
            batch(0, True)
            with pe.Fori(1, NB - 1) as b:
                batch(b, True)
            batch(NB - 1, False)


_INS = ['x', 'fside_BxSxS_0', 'cond_512', 'L0_cond_w', 'L0_cond_u', 'L0_ffn_gate_w', 'L0_ffn_up_w', 'L0_ffn_down_w',
        'L1_cond_w', 'L1_cond_u', 'L1_ffn_router_w', 'L1_ffn_Wa', 'L1_ffn_Wb']


def kernel(**inputs):
    import numpy as _np
    import concourse.bacc as _bacc
    from concourse import mybir as _mybir
    from concourse.bass_utils import run_bass_kernel_spmd as _run

    nc = _bacc.Bacc("TRN2", target_bir_lowering=False, num_devices=1)
    arrays, args = {}, []
    for name in _INS:
        a = _np.ascontiguousarray(inputs[name])
        arrays[f"in_{name}_dram"] = a
        args.append(nc.dram_tensor(f"in_{name}_dram", a.shape, _mybir.dt.from_np(a.dtype), kind="ExternalInput").ap())
    shape = inputs["x"].shape
    args.append(nc.dram_tensor("out_0_dram", shape, _mybir.dt.float32, kind="ExternalOutput").ap())
    adaln_ffn(nc, *args)
    r = _run(nc, [arrays], core_ids=[0])
    return r.results[0]["out_0_dram"]
```

```python
import math
from contextlib import ExitStack

import numpy as np

import concourse.bass as bass
from concourse import mybir

FP32 = mybir.dt.float32
FP16 = mybir.dt.float16
FP8R = mybir.dt.float8e5
ALU = mybir.AluOpType
ACT = mybir.ActivationFunctionType
AX = mybir.AxisListType


HALF, BACK = 2, 3
Y_AT = (7, 5, 3, 1)


def weight_units(q):
    return [("w", m, q, r) for m in range(3) for r in range(4)]


def with_conditioner(units, begins, ends):
    return [(unit, (begins.get(k), ends.get(k))) for k, unit in enumerate(units)]


def first_steps():
    weights = weight_units(0)
    return with_conditioner(weights[:10] + [("y", 0), weights[10], ("y", 1), weights[11], ("y", 2), ("y", 3)],
                            {2 * c: c for c in range(4)}, {2 * c + 2: c for c in range(4)})


def batch_steps(weights, following):
    units = []
    for q in range(4):
        more = weight_units(q + 1) if weights and q < 3 else []
        for i in range(4):
            units += [("h", q, i)] + more[3 * i:3 * i + 3]
            if following and q == 3:
                units.append(("y", i))
    at = [k for k, unit in enumerate(units) if unit[0] == "h"]
    begins = {at[3 * c]: c for c in range(4)}
    ends = {k + 2: c for k, c in begins.items()} if weights else {at[3]: 0, at[6]: 1, at[9]: 2, at[11]: 3}
    return with_conditioner(units, begins, ends)


def products(steps):
    plan = {k: [] for k in range(len(steps))}
    at = [k for k, (unit, _) in enumerate(steps) if unit[0] == "h"]
    nexts = at[1:] + ([len(steps)] if steps[-1][0][0] == "y" else [])
    for n, k in enumerate(nexts):
        if not at:
            gate, up = k - 2, k - 1
        elif n % 4 < 3:
            gate, up = at[n], min(at[n] + 1, k - 1)
        else:
            gate, up = max(at[n], k - 2), k - 1
        plan[gate].append(("gate", n + 1 if at else 16))
        plan[up].append(("up", n + 1 if at else 16))
    return plan


def adaln_ffn(nc, x, f, cond, w0, u0, gate_w, up_w, down_w, w1, u1, router_w, moe_a, moe_b, out):
    NB, T, C = x.shape
    P = 128
    KC = C // P
    NT = T // P
    I = gate_w.shape[0]
    NQ = I // 512
    NE, _, RANK = moe_a.shape
    BLK = 32
    NBLK = 512 // BLK
    assert (NT, KC, NQ, RANK) == (4, 4, 4, P)

    FP8_MAX = 448.0
    EPS = 1e-30
    E30 = float(np.exp(np.float32(30.0)))
    DOWN20 = 2.0 ** -20
    LEAST = 1.125 * 2.0 ** -6
    KY, KW, KH, KM = 8, 10, 10, 8
    KCW = 14

    PRO = first_steps()
    HEAD = batch_steps(True, True)
    MID = batch_steps(False, True)
    LAST = batch_steps(False, False)
    U_HEAD = len(PRO)
    U_MID = U_HEAD + len(HEAD)
    LM = len(MID)

    def units_before(b):
        return U_HEAD if isinstance(b, int) and b == 0 else (b - 1) * LM + U_MID

    x_t = x.rearrange("b (t p) c -> b p t c", p=P)
    f_t = f.rearrange("b (t p) c -> b p t c", p=P)
    out_t = out.rearrange("b (t p) c -> b p t c", p=P)
    x1_dram = nc.dram_tensor("x1_dram", [NB, P, NT, C], FP32, kind="Internal").ap()
    moe_a_v = moe_a.rearrange("e (k p) r -> p k e r", p=P)
    moe_b_v = moe_b.rearrange("e r c -> r e c")
    router_v = router_w.rearrange("(k p) e -> p k e", p=P)
    w_drams = (gate_w, up_w, down_w)

    ctx = ExitStack()
    with ctx:
        def sb(name, shape, dt=FP32):
            return ctx.enter_context(nc.sbuf_tensor(name, shape, dt))

        def sem(name):
            return ctx.enter_context(nc.semaphore(name))

        wg = sb("wg", [P, 2, NQ, KC, 512], FP16)
        wu = sb("wu", [P, 2, NQ, KC, 512], FP16)
        wd = sb("wd", [P, 2, NQ, 4, C], FP16)
        f_nat = sb("f_nat", [P, NT, C])
        x_nat = sb("x_nat", [P, NT, C])
        x_res = sb("x_res", [P, NT, C])
        fT = sb("fT", [P, T])
        th = sb("th", [P, 2, T])
        ek = sb("ek", [P, 2, T])
        eu = sb("eu", [P, T])
        ekv = sb("ekv", [P, T])
        fwd_n = sb("fwd_n", [P, T])
        fwd_d = sb("fwd_d", [P, T])
        rd = sb("rd", [P, T])
        num = sb("num", [P, T])
        y_ch = sb("y_ch", [P, KC, T])
        yT = sb("yT", [P, 2, KC, T], FP16)
        hT = sb("hT", [P, 2, 2, KC, P], FP16)
        src = sb("src", [P, 4, 512])
        qp = sb("qp", [P, 4, 512])
        rc = sb("rc", [P, 2, 512], FP8R)
        rr = sb("rr", [P, 4, 512])
        silu = sb("silu", [P, 2, 512])
        amax = sb("amax", [P, 2, NBLK])
        scale = sb("scale", [P, 4, NBLK])
        rinv = sb("rinv", [P, 4, NBLK])
        ident = sb("ident", [P, P])
        cond_sb = sb("cond_sb", [P, NB, P])
        csum = sb("csum", [P, NB])
        tf = sb("tf", [P, NB])
        half = sb("half", [P, NB])
        ncb = sb("ncb", [P, NB])
        wv = sb("wv", [P, 2, KC])
        uv = sb("uv", [P, 2, KC])
        ew = sb("ew", [P, 2, KC])
        dw = sb("dw", [P, 2, KC])
        dec = sb("dec", [P, 2, KC, NB])
        kb = sb("kb", [P, 2, KC, NB])
        gb = sb("gb", [P, 2, KC, NB])
        tmp1 = sb("tmp1", [P, 2, KC, NB])
        tmp2 = sb("tmp2", [P, 2, KC, NB])
        ini = sb("ini", [P, 2])
        nleast = sb("nleast", [P, 1])
        gap = sb("gap", [P, 5])
        def parts_of(w):
            return w[:, :, :, :, :].rearrange("p a q k n -> p a (q k n)")
        wa = parts_of(wg)[:, :, 0:KC * NE * RANK].rearrange("p a (k n) -> p a k n", k=KC)
        wb = parts_of(wu)[:, :, 0:NE * C].rearrange("p a (e n) -> p a e n", e=NE)

        def raw_at(w, part, at):
            return parts_of(w)[:, part, at:at + 2048].bitcast(FP32)
        wa_raw = [raw_at(w, part, 4096) for w in (wg, wu) for part in range(2)]
        wb_raw = [raw_at(wd, 0, 0), raw_at(wd, 0, 2048), raw_at(wd, 0, 4096), raw_at(wd, 1, 0)]
        def last_quarter(w, part):
            return parts_of(w)[:, part, 6144:8192]
        ek_moe = [last_quarter(wg, c // 2).bitcast(FP32)[:, T * (c % 2):T * (c % 2) + T] for c in range(KC)]
        f_moe = [last_quarter(wu, c // 2).bitcast(FP32)[:, T * (c % 2):T * (c % 2) + T] for c in range(KC)]
        x_moe = rr
        mT = parts_of(wd)[:, :, 6144:8192].rearrange("p a (s t) -> p a s t", s=4)

        def chunk_buffers(c, moe):
            return (ek_moe[c], f_moe[c], src[:, c, :]) if moe else (ek[:, c % 2, :], fT[:, :], eu[:, :])
        def squares_in(b):
            return x_nat if isinstance(b, int) and b == 0 else src
        cbs = silu
        ms = qp
        rw = sb("rw", [P, KC, NE + 1])
        ones = sb("ones", [P, NE + 1])
        onehot = y_ch[0:NE, 0:2, :].rearrange("e k (g p) -> e (k g) p", p=P)
        onehot16 = sb("onehot16", [NE, NE, P], FP16)
        cw = sb("cw", [NE, 2, T], FP16)
        lower = sb("lower", [P, NE, NE])
        ssq = sb("ssq", [P, NT])
        nrm = sb("nrm", [P, NT])
        nr1 = sb("nr1", [P, NT])
        nr2 = sb("nr2", [P, NT])
        lg = sb("lg", [P, NT, NE])
        mx = sb("mx", [P, NT])
        pe_ = sb("pe_", [P, NT, NE])
        zz = sb("zz", [P, NT])
        gt = sb("gt", [P, NT, NE, NE])
        eq = sb("eq", [P, NT, NE, NE])
        cnt = sb("cnt", [P, NT, NE])
        cmb = sb("cmb", [P, NT, NE])
        cmbT = sb("cmbT", [NE + 1, T])

        def bank(name):
            return ctx.enter_context(nc.psum_tensor(name, [P, 512], FP32))
        ps_gate, ps_up, ps_t, ps_m = bank("ps_gate"), bank("ps_up"), bank("ps_t"), bank("ps_m")
        ps_o = [bank(f"ps_o{i}") for i in range(NT)]

        s_const = sem("s_const")
        s_cond = sem("s_cond")
        s_par = sem("s_par")
        s_csum = sem("s_csum")
        s_tf = sem("s_tf")
        s_prep = sem("s_prep")
        s_dw = sem("s_dw")
        s_wload = [sem(f"s_wload{i}") for i in range(4)]
        s_fnat = sem("s_fnat")
        s_xnat = sem("s_xnat")
        s_xres = sem("s_xres")
        s_x1out = sem("s_x1out")
        s_ftr = sem("s_ftr")
        s_xtr = sem("s_xtr")
        s_fT = sem("s_fT")
        s_th = sem("s_th")
        s_ek = sem("s_ek")
        s_eu = sem("s_eu")
        s_min = sem("s_min")
        s_cd = sem("s_cd")
        s_ce = sem("s_ce")
        s_ln = sem("s_ln")
        s_rd = sem("s_rd")
        s_ytr = sem("s_ytr")
        s_ysrc = sem("s_ysrc")
        s_gate = sem("s_gate")
        s_up = sem("s_up")
        s_silu = sem("s_silu")
        s_h = sem("s_h")
        s_amax = sem("s_amax")
        s_scale = sem("s_scale")
        s_rinv = sem("s_rinv")
        s_qp = sem("s_qp")
        s_rc = sem("s_rc")
        s_rr = sem("s_rr")
        s_qt = sem("s_qt")
        s_pu = sem("s_pu")
        s_nq = sem("s_nq")
        s_deq = sem("s_deq")
        s_tr = sem("s_tr")
        s_hi = sem("s_hi")
        s_lo = sem("s_lo")
        s_down = sem("s_down")
        s_x1 = sem("s_x1")
        s_wa = [sem(f"s_wa{k}") for k in range(4)]
        s_wb = [sem(f"s_wb{k}") for k in range(4)]
        s_rwl = sem("s_rwl")
        s_whi = sem("s_whi")
        s_wlo = sem("s_wlo")
        s_yhi = sem("s_yhi")
        s_ylo = sem("s_ylo")
        s_sq = sem("s_sq")
        s_lgt = sem("s_lgt")
        s_rt = sem("s_rt")
        s_rc2 = sem("s_rc2")
        s_lns = sem("s_lns")
        s_ltr = sem("s_ltr")
        s_rsq = sem("s_rsq")
        s_sqa = sem("s_sqa")
        s_sqs = sem("s_sqs")
        s_lgc = sem("s_lgc")
        s_tn = sem("s_tn")
        s_y1 = sem("s_y1")
        s_exp = sem("s_exp")
        s_ctr = sem("s_ctr")
        s_oh = sem("s_oh")
        s_cT = sem("s_cT")
        s_cl = sem("s_cl")
        s_cb = sem("s_cb")
        s_cbs = sem("s_cbs")
        s_e1 = sem("s_e1")
        s_m = sem("s_m")
        s_mhi = sem("s_mhi")
        s_mlo = sem("s_mlo")
        s_e2 = sem("s_e2")
        s_out = sem("s_out")
        s_outd = sem("s_outd")

        SQUARES_AT = 5
        NCD, NCE, NPU = 9, 4, 3
        NRT = 15

        def part_of(unit, k, part):
            if unit[0] == "w":
                _, m, q, r = unit
                return (wg, wu, wd)[m][:, part, q, :, P * r:P * r + P]
            if unit[0] == "y":
                return yT[:, part, :, P * unit[1]:P * unit[1] + P]
            n = 4 * unit[1] + unit[2]
            return hT[:, n % 2, part, :, :]

        tail0, tail = ([unit for unit, _ in steps[-BACK:]] for steps in (PRO, MID))
        assert tail == [unit for unit, _ in HEAD[-BACK:]]
        power_of = {"w": KW, "y": KY, "h": KH}

        block = ctx.enter_context(nc.Block())

        @block.sync
        def _(sp):
            def load_weight(u, unit):
                _, m, q, r = unit
                if u >= 4:
                    sp.wait_ge(s_qp, u - 3)
                rows = w_drams[m][P * (4 * q + r):P * (4 * q + r + 1), :] if m < 2 else \
                    w_drams[m][P * r:P * (r + 1), 512 * q:512 * (q + 1)]
                sp.dma_start(src[:, u % 4, :], rows).then_inc(s_wload[u % 4], 16)

            def load_cond(j, b, source):
                if not (isinstance(j, int) and j == 0):
                    sp.wait_ge(s_ftr, j * KC)
                    sp.wait_ge(s_xtr, j * KC)
                sp.dma_start(f_nat[:, :, :], f_t[b]).then_inc(s_fnat, 16)
                sp.dma_start(x_nat[:, :, :], source[b]).then_inc(s_xnat, 16)

            def load_residual(j, b, source, done, value):
                if done is not None:
                    sp.wait_ge(done, value)
                sp.dma_start(x_res[:, :, :], source[b]).then_inc(s_xres, 16)

            sp.dma_start(cond_sb[:, :, :], cond.rearrange("(a b) d -> a b d", a=1).to_broadcast([P, NB, P]))\
                .then_inc(s_cond, 16)
            units = [unit for unit, _ in PRO + HEAD]
            for u in range(2):
                load_weight(u, units[u])
            for n, (w, u) in enumerate(((w0, u0), (w1, u1))):
                sp.dma_start(wv[:, n, :], w.rearrange("(k p) -> p k", p=P),
                             allow_slow_non_contiguous=True).then_inc(s_par, 16)
                sp.dma_start(uv[:, n, :], u.rearrange("(k p) -> p k", p=P),
                             allow_slow_non_contiguous=True).then_inc(s_par, 16)
            load_cond(0, 0, x_t)
            for u in range(2, 4):
                load_weight(u, units[u])
            load_residual(0, 0, x_t, None, 0)
            for u in range(4, U_MID):
                if u == U_HEAD:
                    load_cond(1, 1, x_t)
                if units[u][0] == "w":
                    load_weight(u, units[u])
            sp.wait_ge(s_const, 7)
            sp.dma_start(rw[:, :, 0:NE], router_v).then_inc(s_rwl, 16)

            def keep_x1(b):
                sp.wait_ge(s_x1, b * NT + NT)
                sp.dma_start(x1_dram[b], x_res[:, :, :]).then_inc(s_x1out, 16)

            with sp.Fori(1, NB - 1) as b:
                load_cond(b + 1, b + 1, x_t)
                keep_x1(b - 1)
                load_residual(b, b, x_t, s_x1out, b * 16)
            load_cond(NB, 0, x1_dram)
            keep_x1(NB - 2)
            load_residual(NB - 1, NB - 1, x_t, s_x1out, 16 * (NB - 1))
            sp.wait_ge(s_up, 16 * NB - 4)
            for k in range(KC):
                sp.dma_start(wa_raw[k].rearrange("p (e r) -> p e r", e=NE), moe_a_v[:, k, :, :]).then_inc(s_wa[k], 16)
            sp.wait_ge(s_down, 16 * NB - 4)
            for k in range(4):
                sp.dma_start(wb_raw[k].rearrange("p (e c) -> p e c", e=2), moe_b_v[:, 2 * k:2 * k + 2, :])\
                    .then_inc(s_wb[k], 16)
            sp.wait_ge(s_lgt, 1)
            load_cond(NB + 1, 1, x1_dram)
            keep_x1(NB - 1)
            load_residual(NB, 0, x1_dram, s_x1out, 16 * NB)

            def store_out(b):
                sp.wait_ge(s_out, b * NT + NT)
                sp.dma_start(out_t[b], x_res[:, :, :]).then_inc(s_outd, 16)

            with sp.Fori(0, NB - 2) as b:
                load_cond(b + (NB + 2), b + 2, x1_dram)
                store_out(b)
                load_residual(b, b + 1, x1_dram, s_outd, b * 16 + 16)
            store_out(NB - 2)
            load_residual(NB - 1, NB - 1, x1_dram, s_outd, 16 * (NB - 1))
            store_out(NB - 1)
            sp.wait_ge(s_outd, 16 * NB)

        @block.gpsimd
        def _(pool):
            nc.gpsimd.memset(ident[:, :], 0.0).then_inc(s_const, 1)
            nc.gpsimd.memset(rw[:, :, :], 0.0)
            nc.gpsimd.memset(ones[:, :], 0.0).then_inc(s_const, 1)
            nc.gpsimd.memset(onehot[:, :, :], 0.0).then_inc(s_const, 1)
            nc.gpsimd.memset(lower[:, :, :], 1.0).then_inc(s_const, 1)
            pool.wait_ge(s_const, 4)
            nc.gpsimd.memset(ones[:, NE:NE + 1], 1.0)
            nc.gpsimd.affine_select(out=ident[:, :], in_=ident[:, :], compare_op=ALU.not_equal, fill=1.0,
                                    base=0, pattern=[[-1, P]], channel_multiplier=1).then_inc(s_const, 1)
            nc.gpsimd.affine_select(out=onehot[:, :, :], in_=onehot[:, :, :], compare_op=ALU.not_equal, fill=1.0,
                                    base=0, pattern=[[-1, NE], [0, P]], channel_multiplier=1).then_inc(s_const, 1)
            nc.gpsimd.affine_select(out=lower[:, :, :], in_=lower[:, :, :], compare_op=ALU.is_gt, fill=0.0,
                                    base=0, pattern=[[1, NE], [-1, NE]], channel_multiplier=0).then_inc(s_const, 1)

            def blocks(ap):
                return ap.rearrange("p (n k) -> p n k", k=BLK)

            def spread(ap):
                return ap.unsqueeze(2).to_broadcast([P, NBLK, BLK])

            def normalise(u, k, unit):
                pool.wait_ge(s_rinv, u + 1)
                if not (isinstance(u, int) and u < 4):
                    pool.wait_ge(s_tr, u - 3)
                nc.gpsimd.tensor_tensor(blocks(qp[:, k % 4, :]), blocks(src[:, k % 4, :]),
                                        spread(rinv[:, k % 4, :]), ALU.mult).then_inc(s_qp, 1)

            def dequantise(u, k):
                pool.wait_ge(s_nq, u + 1)
                at = blocks(qp[:, k % 4, :])
                nc.gpsimd.tensor_tensor(at, at, spread(scale[:, k % 4, :]), ALU.mult).then_inc(s_deq, 1)

            def cond_ekv(j, c, moe=False):
                e, f_, _ = chunk_buffers(c, moe)
                pool.wait_ge(s_min, j + 1)
                nc.gpsimd.tensor_tensor(ekv[:, :], e, f_, ALU.mult).then_inc(s_pu, 1)

            def limit_eu(j, c, moe=False):
                eu_ = chunk_buffers(c, moe)[2]
                pool.wait_ge(s_eu, j + 1)
                if not isinstance(j, int):
                    nc.gpsimd.tensor_tensor(gap[:, 4:5], nleast[:, 0:1], nleast[:, 0:1], ALU.add)
                nc.gpsimd.tensor_scalar(eu_, eu_, E30, None, ALU.min).then_inc(s_pu, 1)

            def cond_euf(j, c, moe=False):
                _, f_, eu_ = chunk_buffers(c, moe)
                pool.wait_ge(s_pu, j * NPU + 2)
                nc.gpsimd.tensor_tensor(f_, eu_, f_, ALU.mult).then_inc(s_pu, 1)

            def run(steps, base, k0, j0, also={}):
                for k, (unit, _) in enumerate(steps):
                    if k0 + k >= HALF:
                        dequantise(base + (k - HALF), k0 + k - HALF)
                    normalise(base + k, k0 + k, unit)
                    begun = steps[k - 1][1][0] if k > 0 else None
                    if begun is not None:
                        cond_ekv(j0 + begun, begun)
                        limit_eu(j0 + begun, begun)
                        cond_euf(j0 + begun, begun)
                    for step in also.get(k, ()):
                        step()

            run(PRO, 0, 0, 0)
            run(HEAD, U_HEAD, U_HEAD, KC)
            with pool.Fori(1, NB - 1) as b:
                run(MID, units_before(b), U_MID, b * KC + KC)
            uL = units_before(NB - 1)
            def low(b, e):
                pool.wait_ge(s_mhi, b * NE + (e + 1))
                nc.gpsimd.tensor_tensor(mT[:, 1, e % 4, :], ms[:, e % 4, :], mT[:, 0, e % 4, :], ALU.subtract)\
                    .then_inc(s_mlo, 1)

            def sum_squares(b):
                sq = squares_in(b)
                pool.wait_ge(s_sq, b + 1)
                nc.gpsimd.tensor_tensor(sq[:, 0:2, :], sq[:, 0:2, :], sq[:, 2:4, :], ALU.add).then_inc(s_sqa, 1)
                pool.wait_ge(s_sqa, b + 1)
                nc.gpsimd.tensor_tensor(sq[:, 0, :], sq[:, 0, :], sq[:, 1, :], ALU.add).then_inc(s_sqs, 1)

            def experts(b, following):
                for e in range(NE):
                    begun = ((b + (NB + 1)) * KC + e, e, True) if following and e < KC else None
                    if begun is not None:
                        limit_eu(*begun)
                        cond_ekv(*begun)
                    low(b, e)
                    if begun is not None:
                        cond_euf(*begun)
                    if following and e == SQUARES_AT:
                        sum_squares(b + 1)

            run(LAST, uL, U_MID, NB * KC, {13: [lambda: sum_squares(0)]})
            for n in range(16 - HALF, 16):
                dequantise(uL + n, U_MID + n)

            experts(0, True)
            with pool.Fori(1, NB - 1) as b:
                experts(b, True)
            experts(NB - 1, False)

        @block.scalar
        def _(act):
            act.wait_ge(s_const, 7)
            nc.scalar.activation(onehot16[:, :, :], onehot[:, :, :], ACT.Copy).then_inc(s_oh, 1)
            act.wait_ge(s_csum, 1)
            nc.scalar.activation(tf[:, :], csum[:, :], ACT.Sigmoid).then_inc(s_tf, 1)
            act.wait_ge(s_par, 4 * 16)
            nc.scalar.activation(ew[:, :, :], wv[:, :, :], ACT.Exp).then_inc(s_dw, 1)
            act.wait_ge(s_dw, 1)
            nc.scalar.activation(dw[:, :, :], ew[:, :, :], ACT.Exp, scale=-1.0).then_inc(s_dw, 1)

            def cond_x(j, c):
                act.wait_ge(s_ftr, j + 1)
                if not (isinstance(j, int) and j == 0):
                    act.wait_ge(s_cd, j * NCD)
                nc.scalar.activation(fT[:, :], ps_m[:, :], ACT.Copy).then_inc(s_fT, 1)

            def cond_tanh(j, c):
                act.wait_ge(s_xtr, j + 1)
                nc.scalar.activation(th[:, c % 2, :], ps_m[:, :], ACT.Tanh, scale=0.5).then_inc(s_th, 1)

            def cond_e(layer, j, c):
                act.wait_ge(s_fT, j + 1)
                nc.scalar.activation(ek[:, c % 2, :], fT[:, :], ACT.Exp).then_inc(s_ek, 1)
                nc.scalar.activation(eu[:, :], fT[:, :], ACT.Exp, bias=uv[:, layer, c:c + 1]).then_inc(s_eu, 1)

            def cond_ln(j, c):
                nc.scalar.preload_act_table_set("natural_log_exp_and_others")
                act.wait_ge(s_cd, j * NCD + 8)
                nc.scalar.activation(rd[:, :], ek[:, c % 2, :], ACT.Ln).then_inc(s_ln, 1)
                act.wait_ge(s_ln, j + 1)
                nc.scalar.activation(rd[:, :], rd[:, :], ACT.Exp, scale=-1.0).then_inc(s_rd, 1)

            def high(u, k, unit, g0):
                act.wait_ge(s_tr, u + 1)
                if unit[0] == "h":
                    n = 4 * unit[1] + unit[2]
                    if not (isinstance(g0, int) and g0 + n < 2):
                        act.wait_ge(s_down, g0 + n - 1)
                nc.scalar.activation(part_of(unit, k, 0), ps_t[:, :].rearrange("p (k t) -> p k t", k=4), ACT.Copy,
                                     scale=-(2.0 ** power_of[unit[0]]))\
                    .then_inc(s_hi, 1)

            def carry(u, column):
                if not isinstance(u, int):
                    nc.scalar.activation(gap[:, column:column + 1], nleast[:, 0:1], ACT.Copy)

            def round_constant(u, k):
                act.wait_ge(s_qp, u + 1)
                carry(u, 2 * (k % 2))
                nc.scalar.activation(rc[:, k % 2, :], qp[:, k % 4, :], ACT.Abs, scale=0.9375 / DOWN20,
                                     saturate=False).then_inc(s_rc, 1)
                act.wait_ge(s_rc, u + 1)
                carry(u, 2 * (k % 2) + 1)
                nc.scalar.activation(rr[:, k % 4, :], rc[:, k % 2, :], ACT.Relu, scale=1.125, bias=nleast[:, 0:1])\
                    .then_inc(s_rr, 1)

            def own(u, k, unit, g0, y0):
                if unit[0] == "h":
                    n = 4 * unit[1] + unit[2]
                    act.wait_ge(s_gate, g0 + n + 1)
                    if not (isinstance(g0, int) and g0 + n < 2):
                        act.wait_ge(s_h, g0 + n - 1)
                    nc.scalar.activation(silu[:, n % 2, :], ps_gate[:, :], ACT.Silu, scale=2.0 ** -(KY + KW))\
                        .then_inc(s_silu, 1)
                if unit[0] == "y":
                    act.wait_ge(s_ytr, y0 + unit[1] + 1)
                    act.wait_ge(s_qp, u - 3)
                    nc.scalar.activation(src[:, k % 4, :], ps_m[:, :], ACT.Copy).then_inc(s_ysrc, 1)

            def run(steps, base, k0, before, g0, y0, j0, layer=0, also={}):
                units = before + [unit for unit, _ in steps]
                nb = len(before)
                for k, (unit, (begins, ends)) in enumerate(steps):
                    y_late = steps[0][0][0] == "h"
                    if unit[0] == "h" or unit[0] == "y" and not y_late:
                        own(base + k, k0 + k, unit, g0, y0)
                    if k0 + k >= BACK:
                        high(base + (k - BACK), k0 + k - BACK, units[nb + k - BACK], g0 if k >= BACK else g0 - 16)
                    if k0 + k >= 1:
                        round_constant(base + (k - 1), k0 + k - 1)
                    if unit[0] == "y" and y_late:
                        own(base + k, k0 + k, unit, g0, y0)
                    c = steps[k - 1][1][0] if k > 0 else None
                    if c is not None:
                        cond_tanh(j0 + c, c)
                    if begins is not None:
                        cond_x(j0 + begins, begins)
                    if ends is not None:
                        cond_ln(j0 + ends, ends)
                    if begins is not None:
                        cond_e(layer, j0 + begins, begins)
                    for step in also.get(k, ()):
                        step()

            run(PRO, 0, 0, [], 0, 0, 0)
            run(HEAD, U_HEAD, U_HEAD, tail0, 0, 4, 4)
            with act.Fori(1, NB - 1) as b:
                run(MID, units_before(b), U_MID, tail, b * 16, b * 4 + 4, b * 4 + 4)
            uL, gL = units_before(NB - 1), 16 * (NB - 1)

            def split_high(dst, raw, landed):
                act.wait_ge(landed, 16)
                nc.scalar.activation(dst, raw, ACT.Copy, scale=2.0 ** KM).then_inc(s_whi, 1)

            def split_a(k):
                split_high(wa[:, 0, k, :], wa_raw[k], s_wa[k])

            def split_b(k):
                split_high(wb[:, 0, 2 * k:2 * k + 2, :].rearrange("p e n -> p (e n)"), wb_raw[k], s_wb[k])

            def squares(b, at_last):
                if at_last:
                    act.wait_ge(s_y1, b)
                else:
                    act.wait_ge(s_ce, (b + NB + 1) * KC * NCE)
                nc.scalar.activation(squares_in(b)[:, :, :], y_ch[:, :, :], ACT.Square).then_inc(s_sq, 1)

            def y_high(b):
                nc.scalar.activation(yT[:, 0, :, :], y_ch[:, :, :], ACT.Copy, scale=2.0 ** KM).then_inc(s_yhi, 1)

            def logits_copy(b):
                act.wait_ge(s_lgt, b + 1)
                nc.scalar.activation(cmbT[:, :], ps_m[0:NE + 1, :], ACT.Copy).then_inc(s_lgc, 1)

            def router(b):
                act.wait_ge(s_rt, b * NRT + 1)
                nc.scalar.activation(nr2[:, :], ssq[:, :], ACT.Ln).then_inc(s_lns, 1)
                act.wait_ge(s_lns, b + 1)
                nc.scalar.activation(nrm[:, :], nr2[:, :], ACT.Exp, scale=-0.5).then_inc(s_rsq, 1)
                act.wait_ge(s_rt, b * NRT + 7)
                nc.scalar.activation(pe_[:, :, :], lg[:, :, :], ACT.Exp).then_inc(s_exp, 1)

            def weights_copy(b):
                act.wait_ge(s_ctr, b + 1)
                nc.scalar.activation(cw[:, 0, :], ps_m[0:NE, :], ACT.Copy, scale=2.0 ** KCW).then_inc(s_cT, 1)

            def spread_copy(b, e):
                act.wait_ge(s_cb, b * NE + (e + 1))
                if e >= 2 or not (isinstance(b, int) and b == 0):
                    act.wait_ge(s_m, b * NE + (e - 1))
                nc.scalar.activation(cbs[:, e % 2, :], ps_t[:, :], ACT.Copy).then_inc(s_cbs, 1)

            def expert_high(b, e):
                act.wait_ge(s_m, b * NE + (e + 1))
                if e >= 4 or not (isinstance(b, int) and b == 0):
                    act.wait_ge(s_e2, b * NE + (e - 3))
                elif e == 0:
                    act.wait_ge(s_down, 16 * NB)
                nc.scalar.activation(mT[:, 0, e % 4, :], ms[:, e % 4, :], ACT.Copy).then_inc(s_mhi, 1)

            def moe_x(j, c):
                act.wait_ge(s_xtr, j + 1)
                nc.scalar.activation(x_moe[:, c, :], ps_m[:, :], ACT.Copy).then_inc(s_th, 1)

            def moe_f(j, c):
                act.wait_ge(s_ftr, j + 1)
                ek_, f_, eu_ = chunk_buffers(c, True)
                nc.scalar.activation(f_, (ps_m if c else ps_t)[:, :], ACT.Copy).then_inc(s_fT, 1)
                act.wait_ge(s_fT, j + 1)
                nc.scalar.activation(ek_, f_, ACT.Exp).then_inc(s_ek, 1)
                nc.scalar.activation(eu_, f_, ACT.Exp, bias=uv[:, 1, c:c + 1]).then_inc(s_eu, 1)

            def moe_ln(j, c):
                act.wait_ge(s_cd, j * NCD + 8)
                act.wait_ge(s_ce, j * NCE - 1)
                nc.scalar.activation(rd[:, :], ek_moe[c], ACT.Ln).then_inc(s_ln, 1)
                act.wait_ge(s_ln, j + 1)
                nc.scalar.activation(rd[:, :], rd[:, :], ACT.Exp, scale=-1.0).then_inc(s_rd, 1)

            def experts(b, following):
                j = (b + (NB + 1)) * KC
                if following:
                    moe_f(j, 0)
                weights_copy(b)
                spread_copy(b, 0)
                for e in range(NE):
                    if following and e < KC:
                        moe_x(j + e, e)
                    if e + 1 < NE:
                        spread_copy(b, e + 1)
                    if following and 1 <= e <= KC:
                        moe_ln(j + (e - 1), e - 1)
                    if following and e == NE - 1:
                        logits_copy(b + 1)
                    expert_high(b, e)
                    if following and e < KC - 1:
                        moe_f(j + (e + 1), e + 1)
                    if following and e == SQUARES_AT:
                        squares(b + 1, True)
                    if following and e == KC:
                        nc.scalar.activation(x_moe[:, :, :], x_moe[:, :, :], ACT.Tanh, scale=0.5).then_inc(s_tn, 1)
                        nc.scalar.preload_act_table_set("natural_log_exp_and_others")
                if following:
                    act.wait_ge(s_e1, b * NE + NE)
                    y_high(b + 1)
                    router(b + 1)

            run(LAST, uL, U_MID, tail, gL, 4 * NB, 4 * NB, 1, {
                12: [lambda: squares(0, False)],
                13: [lambda: split_a(0), lambda: split_a(1)],
                14: [lambda: split_a(2), lambda: split_a(3)],
                15: [lambda: logits_copy(0)]})
            high(uL + 13, U_MID + 13, ("h", 3, 1), gL)
            round_constant(uL + 15, U_MID + 15)

            act.wait_ge(s_up, 16 * NB)
            y_high(0)
            split_b(0)
            high(uL + 14, U_MID + 14, ("h", 3, 2), gL)
            split_b(1)
            nc.scalar.preload_act_table_set("natural_log_exp_and_others")
            high(uL + 15, U_MID + 15, ("h", 3, 3), gL)
            router(0)
            split_b(2)
            split_b(3)
            act.wait_ge(s_qp, uL + 16)
            experts(0, True)
            with act.Fori(1, NB - 1) as b:
                experts(b, True)
            experts(NB - 1, False)

        @block.vector
        def _(dve):
            v = nc.vector
            n = [0]

            def link(ins):
                n[0] += 1
                ins.then_inc(s_prep, 1)
                dve.wait_ge(s_prep, n[0])

            v.memset(nleast[:, :], -LEAST).then_inc(s_prep, 1)
            n[0] += 1
            dve.wait_ge(s_cond, 16)
            v.tensor_reduce(csum[:, :], cond_sb[:, :, :], AX.X, ALU.add).then_inc(s_csum, 1)

            def parameters():
                dve.wait_ge(s_tf, 1)
                link(v.tensor_scalar(half[:, :], tf[:, :], 0.5, 0.5, ALU.mult, ALU.add))
                link(v.tensor_scalar(ncb[:, :], tf[:, :], -0.1, -0.4, ALU.mult, ALU.add))
                dve.wait_ge(s_dw, 2)
                for layer in range(2):
                    link(v.tensor_tensor(dec[:, layer], dw[:, layer].unsqueeze(2).to_broadcast([P, KC, NB]),
                                         half[:, :].unsqueeze(1).to_broadcast([P, KC, NB]), ALU.mult))
                link(v.tensor_scalar(tmp1[:, :, :, :], dec[:, :, :, :], -1.0, 1.0, ALU.mult, ALU.add))
                link(v.tensor_scalar(tmp2[:, :, :, :], dec[:, :, :, :], 1.0, None, ALU.add))
                link(v.tensor_tensor(tmp1[:, :, :, :], tmp1[:, :, :, :], tmp2[:, :, :, :], ALU.mult))
                link(v.tensor_scalar(kb[:, :, :, :], tmp1[:, :, :, :], 1e-12, None, ALU.max))
                link(v.reciprocal(tmp2[:, :, :, :], kb[:, :, :, :]))
                link(v.tensor_tensor(gb[:, :, :, :], dec[:, :, :, :], tmp2[:, :, :, :], ALU.mult))

            def cond_a(layer, j, c, b, moe=False):
                at = j * NCD
                e, f_, eu_ = chunk_buffers(c, moe)
                e_back = e[:, ::-1]
                dd = dec[:, layer, c, bass.ds(b, 1)].to_broadcast([P, T])
                g = gb[:, layer, c, bass.ds(b, 1)]
                k = kb[:, layer, c, bass.ds(b, 1)]

                def did(ins):
                    ins.then_inc(s_cd, 1)
                dve.wait_ge(s_min, j + 1)
                did(v.tensor_tensor_scan(fwd_d[:, :], dd, e, 0.0, ALU.mult, ALU.add))
                dve.wait_ge(s_cd, at + 1)
                did(v.tensor_tensor(ini[:, 1:2], fwd_d[:, T - 1:T], g, ALU.mult))
                dve.wait_ge(s_pu, j * NPU + (2 if moe else 1))
                did(v.tensor_tensor_scan(fwd_n[:, :], dd, ekv[:, :], 0.0, ALU.mult, ALU.add))
                dve.wait_ge(s_cd, at + 2)
                did(v.tensor_tensor_scan(e_back, dd, fwd_d[:, ::-1], ini[:, 1:2], ALU.mult, ALU.add))
                dve.wait_ge(s_cd, at + 3)
                did(v.tensor_tensor(ini[:, 0:1], fwd_n[:, T - 1:T], g, ALU.mult))
                dve.wait_ge(s_pu, j * NPU + 2)
                dve.wait_ge(s_cd, at + 4)
                did(v.scalar_tensor_tensor(out=fwd_d[:, :], in0=e, scalar=k, in1=eu_,
                                           op0=ALU.mult, op1=ALU.add))
                dve.wait_ge(s_cd, at + 5)
                did(v.tensor_tensor_scan(ekv[:, ::-1], dd, fwd_n[:, ::-1], ini[:, 0:1], ALU.mult, ALU.add))
                dve.wait_ge(s_cd, at + 6)
                did(v.tensor_scalar(e, fwd_d[:, :], 1e-8, None, ALU.max))
                dve.wait_ge(s_pu, j * NPU + 3)
                if not (isinstance(j, int) and j == 0):
                    dve.wait_ge(s_ce, j * NCE)
                dve.wait_ge(s_cd, at + 7)
                did(v.scalar_tensor_tensor(out=num[:, :], in0=ekv[:, :], scalar=k, in1=f_,
                                           op0=ALU.mult, op1=ALU.add))

            def cond_min(j, c, moe=False):
                e = chunk_buffers(c, moe)[0]
                dve.wait_ge(s_ek, j + 1)
                v.tensor_scalar(e, e, E30, None, ALU.min).then_inc(s_min, 1)

            def quotient(j, c, b, y_free, e, at):
                dve.wait_ge(s_rd, j + 1)
                v.tensor_tensor(e, e, rd[:, :], ALU.mult).then_inc(s_ce, 1)
                dve.wait_ge(s_ce, at)
                v.scalar_tensor_tensor(out=e, in0=e, scalar=2.0, in1=rd[:, :],
                                       op0=ALU.subtract, op1=ALU.mult).then_inc(s_ce, 1)
                dve.wait_ge(s_ce, at + 1)
                if c == 0:
                    y_free()
                return v.scalar_tensor_tensor(out=y_ch[:, c, :], in0=num[:, :], scalar=ncb[:, bass.ds(b, 1)],
                                              in1=e, op0=ALU.mult, op1=ALU.mult)

            def cond_b(layer, j, c, b, y_free):
                dve.wait_ge(s_th, j + 1)
                dve.wait_ge(s_cd, j * NCD + 9)
                v.scalar_tensor_tensor(out=num[:, :], in0=th[:, c % 2, :], scalar=1.0, in1=num[:, :],
                                       op0=ALU.add, op1=ALU.mult).then_inc(s_ce, 1)
                quotient(j, c, b, y_free, ek[:, c % 2, :], j * NCE + 2).then_inc(s_ce, 1)

            def moe_b(j, c, b, y_free):
                dve.wait_ge(s_cd, j * NCD + 9)
                quotient(j, c, b, y_free, ek_moe[c], j * NCE + 1).then_inc(s_ce, 2)

            def blocks(ap):
                return ap.rearrange("p (n k) -> p n k", k=BLK)

            def low(u, k, unit):
                dve.wait_ge(s_hi, u + 1)
                v.scalar_tensor_tensor(out=part_of(unit, k, 1), in0=ps_t[:, :].rearrange("p (k t) -> p k t", k=4),
                                       scalar=-(2.0 ** power_of[unit[0]]), in1=part_of(unit, k, 0),
                                       op0=ALU.mult, op1=ALU.subtract).then_inc(s_lo, 1)

            def round_up(u, k):
                dve.wait_ge(s_rr, u + 1)
                q = qp[:, k % 4, :]
                v.scalar_tensor_tensor(out=q, in0=rr[:, k % 4, :], scalar=LEAST, in1=q,
                                       op0=ALU.add, op1=ALU.add).then_inc(s_qt, 1)

            def round_off(u, k):
                dve.wait_ge(s_qt, u + 1)
                q = qp[:, k % 4, :]
                v.scalar_tensor_tensor(out=q, in0=rr[:, k % 4, :], scalar=LEAST, in1=q,
                                       op0=ALU.add, op1=ALU.subtract).then_inc(s_nq, 1)

            def largest(u, k, unit, g0, y0, loads):
                if unit[0] == "h":
                    m = 4 * unit[1] + unit[2]
                    dve.wait_ge(s_silu, g0 + m + 1)
                    dve.wait_ge(s_up, g0 + m + 1)
                    v.scalar_tensor_tensor(out=src[:, k % 4, :], in0=ps_up[:, :], scalar=2.0 ** -(KY + KW),
                                           in1=silu[:, m % 2, :], op0=ALU.mult, op1=ALU.mult).then_inc(s_h, 1)
                    dve.wait_ge(s_h, g0 + m + 1)
                elif unit[0] == "y":
                    dve.wait_ge(s_ysrc, y0 + unit[1] + 1)
                else:
                    loads[k % 4] += 16
                    dve.wait_ge(s_wload[k % 4], loads[k % 4])
                v.tensor_reduce(amax[:, k % 2, :], blocks(src[:, k % 4, :]), AX.X, ALU.max,
                                apply_absolute_value=True).then_inc(s_amax, 1)

            def scales(u, k):
                dve.wait_ge(s_amax, u + 1)
                if not (isinstance(u, int) and u < 4):
                    dve.wait_ge(s_deq, u - 3)
                v.tensor_scalar(scale[:, k % 4, :], amax[:, k % 2, :], 1.0 / (FP8_MAX * DOWN20), EPS / DOWN20,
                                ALU.mult, ALU.max).then_inc(s_scale, 1)

            def inverses(u, k):
                dve.wait_ge(s_scale, u + 1)
                v.reciprocal(rinv[:, k % 4, :], scale[:, k % 4, :]).then_inc(s_rinv, 1)

            def sum_x1(b, i):
                dve.wait_ge(s_down, b * 16 + (13 + i))
                if i == 0:
                    dve.wait_ge(s_xres, b * 16 + 16)
                v.scalar_tensor_tensor(out=x_res[:, i, :], in0=ps_o[i][:, :], scalar=2.0 ** -(KH + KW),
                                       in1=x_res[:, i, :], op0=ALU.mult, op1=ALU.add).then_inc(s_x1, 1)

            def run(steps, base, k0, before, g0, y0, j0, b, loads, layer=0, y_free=None, sums=None, also={}):
                units = before + [unit for unit, _ in steps]
                nb = len(before)
                for k, (unit, _) in enumerate(steps):
                    n, at = k0 + k, base + k
                    begun, ended = steps[k - 1][1] if k > 0 else (None, None)
                    if n >= HALF:
                        round_up(at - HALF, n - HALF)
                    products_run = unit[0] != "w" and steps[0][0][0] == "h"
                    if products_run:
                        low(at - BACK, n - BACK, units[nb + k - BACK])
                    else:
                        largest(at, n, unit, g0, y0, loads)
                    if n >= HALF:
                        round_off(at - HALF, n - HALF)
                    if products_run:
                        largest(at, n, unit, g0, y0, loads)
                    scales(at, n)
                    if not products_run and n >= BACK:
                        low(at - BACK, n - BACK, units[nb + k - BACK])
                    if begun is not None:
                        cond_min(j0 + begun, begun)
                    inverses(at, n)
                    if sums is not None and k == 2:
                        for i in range(NT):
                            sum_x1(sums, i)
                    if ended is not None:
                        cond_b(layer, j0 + ended, ended, b, y_free)
                    if begun is not None:
                        cond_a(layer, j0 + begun, begun, b)
                    for step in also.get(k, ()):
                        step()

            loads = [0] * 4
            run(PRO, 0, 0, [], 0, 0, 0, 0, loads, y_free=lambda: None, also={0: [parameters]})
            run(HEAD, U_HEAD, U_HEAD, tail0, 0, 4, 4, 1, loads, y_free=lambda: dve.wait_ge(s_ytr, 4))
            with dve.Fori(1, NB - 1) as b:
                run(MID, units_before(b), U_MID, tail, b * 16, b * 4 + 4, b * 4 + 4, b + 1, loads,
                    y_free=lambda: dve.wait_ge(s_ytr, b * 4 + 4), sums=b - 1)
            uL, gL = units_before(NB - 1), 16 * (NB - 1)
            def split_low(dst, raw, high_, n):
                dve.wait_ge(s_whi, n)
                v.scalar_tensor_tensor(out=dst, in0=raw, scalar=2.0 ** KM, in1=high_,
                                       op0=ALU.mult, op1=ALU.subtract).then_inc(s_wlo, 1)

            def split_a(k):
                split_low(wa[:, 1, k, :], wa_raw[k], wa[:, 0, k, :], k + 1)

            def split_b(k):
                e2 = slice(2 * k, 2 * k + 2)
                split_low(wb[:, 1, e2, :].rearrange("p e n -> p (e n)"), wb_raw[k],
                          wb[:, 0, e2, :].rearrange("p e n -> p (e n)"), KC + k + 1)

            def y_low(b):
                dve.wait_ge(s_yhi, b + 1)
                v.scalar_tensor_tensor(out=yT[:, 1, :, :].rearrange("p k t -> p (k t)"),
                                       in0=y_ch[:, :, :].rearrange("p k t -> p (k t)"), scalar=2.0 ** KM,
                                       in1=yT[:, 0, :, :].rearrange("p k t -> p (k t)"),
                                       op0=ALU.mult, op1=ALU.subtract).then_inc(s_ylo, 1)

            def router(b):
                at = b * NRT
                m = [0]

                def did(ins):
                    m[0] += 1
                    ins.then_inc(s_rt, 1)
                    dve.wait_ge(s_rt, at + m[0])
                over_e = [P, NT, NE]
                dve.wait_ge(s_ltr, b + 1)
                lgs = ps_m[:, 0:NT * 16].rearrange("p (i n) -> p i n", n=16)
                did(v.tensor_scalar(ssq[:, :], lgs[:, :, NE], 1e-24, None, ALU.max))
                dve.wait_ge(s_rsq, b + 1)
                did(v.tensor_tensor(nr1[:, :], nrm[:, :], ssq[:, :], ALU.mult))
                did(v.tensor_tensor(nr1[:, :], nr1[:, :], nrm[:, :], ALU.mult))
                did(v.scalar_tensor_tensor(out=nr1[:, :], in0=nr1[:, :], scalar=3.0, in1=nrm[:, :],
                                           op0=ALU.subtract, op1=ALU.mult))
                did(v.scalar_tensor_tensor(out=lg[:, :, :], in0=lgs[:, :, 0:NE], scalar=-0.5,
                                           in1=nr1[:, :].unsqueeze(2).to_broadcast(over_e),
                                           op0=ALU.mult, op1=ALU.mult))
                did(v.tensor_reduce(mx[:, :], lg[:, :, :], AX.X, ALU.max))
                did(v.tensor_tensor(lg[:, :, :], lg[:, :, :], mx[:, :].unsqueeze(2).to_broadcast(over_e),
                                    ALU.subtract))
                dve.wait_ge(s_exp, b + 1)
                did(v.tensor_reduce(zz[:, :], pe_[:, :, :], AX.X, ALU.add))
                did(v.reciprocal(mx[:, :], zz[:, :]))
                did(v.tensor_tensor(pe_[:, :, :], pe_[:, :, :], mx[:, :].unsqueeze(2).to_broadcast(over_e),
                                    ALU.mult))
                mine = pe_[:, :, :].unsqueeze(3).to_broadcast([P, NT, NE, NE])
                theirs = pe_[:, :, :].unsqueeze(2).to_broadcast([P, NT, NE, NE])
                v.tensor_tensor(gt[:, :, :, :], theirs, mine, ALU.is_gt).then_inc(s_rc2, 1)
                v.tensor_tensor(eq[:, :, :, :], theirs, mine, ALU.is_equal).then_inc(s_rc2, 1)
                dve.wait_ge(s_rc2, b * 4 + 2)
                v.tensor_tensor(eq[:, :, :, :], eq[:, :, :, :],
                                lower[:, :, :].unsqueeze(1).to_broadcast([P, NT, NE, NE]), ALU.mult)\
                    .then_inc(s_rc2, 1)
                dve.wait_ge(s_rc2, b * 4 + 3)
                v.tensor_tensor(gt[:, :, :, :], gt[:, :, :, :], eq[:, :, :, :], ALU.add).then_inc(s_rc2, 1)
                dve.wait_ge(s_rc2, b * 4 + 4)
                did(v.tensor_reduce(cnt[:, :, :], gt[:, :, :, :], AX.X, ALU.add))
                did(v.scalar_tensor_tensor(out=cmb[:, :, :], in0=cnt[:, :, :], scalar=1.5, in1=pe_[:, :, :],
                                           op0=ALU.is_lt, op1=ALU.mult))
                did(v.tensor_reduce(zz[:, :], cmb[:, :, :], AX.X, ALU.add))
                did(v.reciprocal(mx[:, :], zz[:, :]))
                did(v.tensor_tensor(cmb[:, :, :], cmb[:, :, :], mx[:, :].unsqueeze(2).to_broadcast(over_e),
                                    ALU.mult))
                assert m[0] == NRT

            ps_e = (ps_gate, ps_up)

            def expert(b, e):
                dve.wait_ge(s_e1, b * NE + (e + 1))
                dve.wait_ge(s_cbs, b * NE + (e + 1))
                if e >= 4 or not (isinstance(b, int) and b == 0):
                    dve.wait_ge(s_mlo, b * NE + (e - 3))
                v.scalar_tensor_tensor(out=ms[:, e % 4, :], in0=ps_e[e % 2][:, :], scalar=2.0 ** -(KM + KCW),
                                       in1=cbs[:, e % 2, :], op0=ALU.mult, op1=ALU.mult).then_inc(s_m, 1)

            def finish(b):
                dve.wait_ge(s_xres, (b + NB) * 16 + 16)
                dve.wait_ge(s_e2, b * NE + NE)
                for i in range(NT):
                    v.scalar_tensor_tensor(out=x_res[:, i, :], in0=ps_o[i][:, :], scalar=2.0 ** -(2 * KM),
                                           in1=x_res[:, i, :], op0=ALU.mult, op1=ALU.add).then_inc(s_out, 1)

            def y_used(b):
                def wait():
                    dve.wait_ge(s_lgt, b + 1)
                    dve.wait_ge(s_ylo, b + 1)
                    dve.wait_ge(s_sq, b + 1)
                return wait

            def weights_low(b):
                dve.wait_ge(s_cT, b + 1)
                v.scalar_tensor_tensor(out=cw[:, 1, :], in0=ps_m[0:NE, :], scalar=2.0 ** KCW, in1=cw[:, 0, :],
                                       op0=ALU.mult, op1=ALU.subtract).then_inc(s_cl, 1)

            def experts(b, following):
                j = (b + (NB + 1)) * KC
                weights_low(b)
                if not (isinstance(b, int) and b == 0):
                    finish(b - 1)
                for e in range(NE):
                    expert(b, e)
                    if following and e < KC:
                        cond_min(j + e, e, True)
                    if following and 1 <= e <= KC:
                        moe_b(j + (e - 1), e - 1, b + 1, y_used(b))
                    if following and e < KC:
                        cond_a(1, j + e, e, b + 1, True)
                    if following and e == KC:
                        dve.wait_ge(s_tn, b + 1)
                        dve.wait_ge(s_ce, (j + KC) * NCE)
                        v.scalar_tensor_tensor(out=y_ch[:, :, :].rearrange("p k t -> p (k t)"),
                                               in0=x_moe[:, :, :].rearrange("p k t -> p (k t)"), scalar=1.0,
                                               in1=y_ch[:, :, :].rearrange("p k t -> p (k t)"),
                                               op0=ALU.add, op1=ALU.mult).then_inc(s_y1, 1)
                if following:
                    y_low(b + 1)
                    router(b + 1)

            run(LAST, uL, U_MID, tail, gL, 4 * NB, 4 * NB, 0, loads, layer=1,
                y_free=lambda: dve.wait_ge(s_ytr, 4 * NB), sums=NB - 2, also={
                    13: [lambda: split_a(0), lambda: split_a(1)], 14: [lambda: split_a(2), lambda: split_a(3)]})

            low(uL + 13, U_MID + 13, ("h", 3, 1))
            for n in (14, 15):
                round_up(uL + n, U_MID + n)
                round_off(uL + n, U_MID + n)
            y_low(0)
            split_b(0)
            low(uL + 14, U_MID + 14, ("h", 3, 2))
            split_b(1)
            sum_x1(NB - 1, 0)
            low(uL + 15, U_MID + 15, ("h", 3, 3))
            router(0)
            split_b(2)
            split_b(3)
            for i in range(1, NT):
                sum_x1(NB - 1, i)
            experts(0, True)
            with dve.Fori(1, NB - 1) as b:
                experts(b, True)
            experts(NB - 1, False)
            finish(NB - 1)

        @block.tensor
        def _(pe):
            t = nc.tensor
            pe.wait_ge(s_const, 7)

            def split_product(bank_, lhs, rhs, nk, first, last, done=None):
                for k in range(nk):
                    for n, (a, c) in enumerate(((0, 0), (0, 1), (1, 0))):
                        ins = t.matmul(bank_, lhs(a, k), rhs(c, k), start=first and k == 0 and n == 0,
                                       stop=last and k == nk - 1 and n == 2)
                if done is not None:
                    ins.then_inc(done, 1)

            def transpose4(bank_, tiles, done):
                for i, tile in enumerate(tiles):
                    ins = t.transpose(bank_[:, P * i:P * i + P], tile, ident[:, :])
                ins.then_inc(done, 1)

            def cond_f(j, c, bank_free, bank_=None):
                if c == 0:
                    pe.wait_ge(s_fnat, (j // KC) * 16 + 16 if isinstance(j, int) else j * 4 + 16)
                bank_free(j)
                transpose4(bank_ or ps_m, [f_nat[:, i, P * c:P * c + P] for i in range(NT)], s_ftr)

            def cond_x(j, c):
                if c == 0:
                    pe.wait_ge(s_xnat, ((j // KC) * 16 + 16) if isinstance(j, int) else j * 4 + 16)
                pe.wait_ge(s_fT, j + 1)
                transpose4(ps_m, [x_nat[:, i, P * c:P * c + P] for i in range(NT)], s_xtr)

            def product(what, g, n):
                q, i = n // 4 % 4, n % 4
                w, bank_, read, done = (wg, ps_gate, s_silu, s_gate) if what == "gate" else (wu, ps_up, s_h, s_up)
                if not (isinstance(g, int) and g == 0):
                    pe.wait_ge(read, g)
                split_product(bank_[:, :], lambda a, k: yT[:, a, k, P * i:P * i + P],
                              lambda c, k: w[:, c, q, k, :], KC, True, True, done)

            def down(u, q, i, b):
                pe.wait_ge(s_lo, u + 1)
                if q == 0 and not (isinstance(b, int) and b == 0):
                    pe.wait_ge(s_x1, (b - 1) * NT + (i + 1))
                n = (4 * q + i) % 2
                split_product(ps_o[i][:, :], lambda a, k: hT[:, n, a, k, :], lambda c, k: wd[:, c, q, k, :],
                              4, q == 0, q == NQ - 1, s_down)

            def parts(u, k):
                pe.wait_ge(s_deq, u + 1)
                if not (isinstance(u, int) and u == 0):
                    pe.wait_ge(s_lo, u)
                transpose4(ps_t, [qp[:, k % 4, P * n:P * n + P] for n in range(4)], s_tr)

            def order_of(unit, k, steps):
                if unit[0] == "w" or steps[0][0][0] == "w":
                    return "parts", "gate", "up", "down"
                if unit[0] == "y":
                    return "up", "parts", "gate", "down"
                if steps[min(k + 1, len(steps) - 1)][0][0] == "w":
                    return "parts", "gate", "down", "up"
                return "gate", "down", "parts", "up"

            def run(steps, base, k0, before, g0, y0, j0, b, ready, also={}):
                units = before + [unit for unit, _ in steps]
                nb = len(before)
                plan = products(steps)

                def y_tile(i):
                    if i == 0:
                        pe.wait_ge(s_ce, (j0 + KC) * NCE)
                        pe.wait_ge(s_th, j0 + KC)
                    else:
                        pe.wait_ge(s_ysrc, y0 + i)
                    transpose4(ps_m, [y_ch[:, c, P * i:P * i + P] for c in range(KC)], s_ytr)

                for k, (unit, (begins, _)) in enumerate(steps):
                    if unit[0] == "y" and steps[0][0][0] == "h":
                        y_tile(unit[1])
                    if begins is not None:
                        def free(j, c=begins):
                            if c > 0:
                                pe.wait_ge(s_th, j)
                            elif not (isinstance(y0, int) and y0 == 0):
                                pe.wait_ge(s_ysrc, y0)
                        cond_f(j0 + begins, begins, free)
                    c = steps[k - 1][1][0] if k > 0 else None
                    if c is not None:
                        cond_x(j0 + c, c)
                    past = units[nb + k - BACK] if k0 + k >= BACK else ("none",)
                    for what in order_of(unit, k, steps):
                        if what == "parts" and k0 + k >= HALF:
                            parts(base + (k - HALF), k0 + k - HALF)
                            if steps[0][0][0] == "w" and steps[min(k + 1, len(steps) - 1)][0][0] == "y" and \
                                    k + 1 < len(steps):
                                y_tile(steps[k + 1][0][1])
                        elif what == "down" and past[0] == "h":
                            down(base + (k - BACK), past[1], past[2], b if k >= BACK else b - 1)
                        else:
                            for kind, n in plan[k]:
                                if kind == what:
                                    if kind == "gate" and n in ready:
                                        pe.wait_ge(s_lo, base + ready[n])
                                    product(what, g0 + n, n)
                    for step in also.get(k, ()):
                        step()

            places = {unit: n for n, (unit, _) in enumerate(HEAD)}
            before = {unit: n for n, (unit, _) in enumerate(PRO)}
            ready_pro = {16: max(before["y", 0], before["w", 1, 0, 3]) + 1}
            ready_head = {i: before["y", i] + 1 - U_HEAD for i in range(1, 4)}
            for q in range(1, NQ):
                ready_head[4 * q] = max(places["w", m, q, r] for m in range(2) for r in range(4)) + 1
            ready_head[16] = len(HEAD) - Y_AT[0] + 1
            ready_mid = {i: 1 - Y_AT[i] for i in range(1, 4)}
            ready_mid[16] = LM - Y_AT[0] + 1

            run(PRO, 0, 0, [], -16, 0, 0, 0, ready_pro)
            run(HEAD, U_HEAD, U_HEAD, tail0, 0, 4, 4, 0, ready_head)
            with pe.Fori(1, NB - 1) as b:
                run(MID, units_before(b), U_MID, tail, b * 16, b * 4 + 4, b * 4 + 4, b, ready_mid)
            uL, gL = units_before(NB - 1), 16 * (NB - 1)
            ps_e = (ps_gate, ps_up)

            def logits(b):
                pe.wait_ge(s_rwl, 16)
                if isinstance(b, int) and b == 0:
                    pe.wait_ge(s_ce, (NB + 1) * KC * NCE)
                else:
                    pe.wait_ge(s_y1, b)
                pe.wait_ge(s_th, (b + (NB + 1)) * KC)
                for k in range(KC):
                    t.matmul(ps_m[0:NE + 1, :], rw[:, k, :], y_ch[:, k, :], start=k == 0, stop=False)

            def norms(b):
                pe.wait_ge(s_sqs, b + 1)
                t.matmul(ps_m[0:NE + 1, :], ones[:, :], squares_in(b)[:, 0, :], start=False, stop=True).then_inc(s_lgt, 1)

            def to_tokens():
                for i in range(NT):
                    ins = t.transpose(ps_m[:, 16 * i:16 * i + NE + 1], cmbT[:, P * i:P * i + P],
                                      ident[0:NE + 1, 0:NE + 1])
                ins.then_inc(s_ltr, 1)

            def combine(b):
                pe.wait_ge(s_rt, b * NRT + NRT)
                for i in range(NT):
                    ins = t.transpose(ps_m[0:NE, P * i:P * i + P], cmb[:, i, :], ident[:, :])
                ins.then_inc(s_ctr, 1)

            def spread(b, e):
                if e == 0:
                    pe.wait_ge(s_cl, b + 1)
                else:
                    pe.wait_ge(s_cbs, b * NE + e)
                t.matmul(ps_t[:, :], onehot16[:, e, :], cw[:, 0, :], start=True, stop=False)
                t.matmul(ps_t[:, :], onehot16[:, e, :], cw[:, 1, :], start=False, stop=True).then_inc(s_cb, 1)

            def first(b, e):
                if e < 2 and isinstance(b, int) and b == 0:
                    pe.wait_ge(s_silu if e == 0 else s_h, 16 * NB)
                else:
                    pe.wait_ge(s_m, b * NE + (e - 1))
                split_product(ps_e[e % 2][:, :], lambda a, k: wa[:, a, k, RANK * e:RANK * e + RANK],
                              lambda c, k: yT[:, c, k, :], KC, True, True, s_e1)

            def second(b, e, tiles=range(NT)):
                pe.wait_ge(s_mlo, b * NE + (e + 1))
                for i in tiles:
                    if e == 0:
                        if isinstance(b, int) and b == 0:
                            pe.wait_ge(s_x1, NB * NT)
                        else:
                            pe.wait_ge(s_out, (b - 1) * NT + (i + 1))
                    for n, (a, c) in enumerate(((0, 0), (0, 1), (1, 0))):
                        ins = t.matmul(ps_o[i][:, :], mT[:, a, e % 4, P * i:P * i + P], wb[:, c, e, :],
                                       start=e == 0 and n == 0, stop=e == NE - 1 and n == 2)
                if i == NT - 1:
                    ins.then_inc(s_e2, 1)

            def batch(b, following):
                j = (b + (NB + 1)) * KC
                if isinstance(b, int) and b == 0:
                    pe.wait_ge(s_lo, uL + 16)
                else:
                    pe.wait_ge(s_cbs, b * NE)
                if following:
                    cond_f(j, 0, lambda j_: None, ps_t)
                if not (isinstance(b, int) and b == 0):
                    pe.wait_ge(s_ylo, b + 1)
                    first(b, 0)
                combine(b)
                if following:
                    pe.wait_ge(s_fT, j + 1)
                spread(b, 0)
                for e in range(NE):
                    if e + 1 < NE:
                        first(b, e + 1)
                        spread(b, e + 1)
                    if following and e < KC:
                        if e == 0:
                            pe.wait_ge(s_cl, b + 1)
                        cond_x(j + e, e)
                    if following and e == NE - 1:
                        pe.wait_ge(s_lgc, b + 2)
                        second(b, e - 1, range(0, 1))
                        to_tokens()
                        second(b, e - 1, range(1, NT))
                    elif e >= 1:
                        second(b, e - 1)
                    if following and e < KC - 1:
                        cond_f(j + (e + 1), e + 1, lambda j_: pe.wait_ge(s_th, j_))
                    if following and e == SQUARES_AT:
                        logits(b + 1)
                    if following and e == SQUARES_AT + 1:
                        norms(b + 1)
                second(b, NE - 1)

            run(LAST, uL, U_MID, tail, gL, 4 * NB, 4 * NB, NB - 1, ready_mid, {
                14: [lambda: logits(0), lambda: norms(0)]})
            parts(uL + 14, U_MID + 14)
            pe.wait_ge(s_lgc, 1)
            to_tokens()
            down(uL + 13, 3, 1, NB - 1)
            parts(uL + 15, U_MID + 15)
            down(uL + 14, 3, 2, NB - 1)
            pe.wait_ge(s_wlo, 4)
            pe.wait_ge(s_ylo, 1)
            first(0, 0)
            down(uL + 15, 3, 3, NB - 1)
            pe.wait_ge(s_wlo, 8)
            batch(0, True)
            with pe.Fori(1, NB - 1) as b:
                batch(b, True)
            batch(NB - 1, False)


_INS = ['x', 'fside_BxSxS_0', 'cond_512', 'L0_cond_w', 'L0_cond_u', 'L0_ffn_gate_w', 'L0_ffn_up_w', 'L0_ffn_down_w',
        'L1_cond_w', 'L1_cond_u', 'L1_ffn_router_w', 'L1_ffn_Wa', 'L1_ffn_Wb']


def kernel(**inputs):
    import numpy as _np
    import concourse.bacc as _bacc
    from concourse import mybir as _mybir
    from concourse.bass_utils import run_bass_kernel_spmd as _run

    nc = _bacc.Bacc("TRN2", target_bir_lowering=False, num_devices=1)
    arrays, args = {}, []
    for name in _INS:
        a = _np.ascontiguousarray(inputs[name])
        arrays[f"in_{name}_dram"] = a
        args.append(nc.dram_tensor(f"in_{name}_dram", a.shape, _mybir.dt.from_np(a.dtype), kind="ExternalInput").ap())
    shape = inputs["x"].shape
    args.append(nc.dram_tensor("out_0_dram", shape, _mybir.dt.float32, kind="ExternalOutput").ap())
    adaln_ffn(nc, *args)
    r = _run(nc, [arrays], core_ids=[0])
    return r.results[0]["out_0_dram"]
```
